# Optimizing a Trainium2 kernel written in Bass

```python
import numpy as np
import jax
import jax.numpy as jnp

def _softmax(x, axis=-1):
    return jax.nn.softmax(x, axis=axis)

def _gelu(x):
    return jax.nn.gelu(x, approximate=True)

def _silu(x):
    return jax.nn.silu(x)

def _sigmoid(x):
    return jax.nn.sigmoid(x)

def _layernorm(x, axis=-1, eps=1e-05):
    m = jnp.mean(x, axis=axis, keepdims=True)
    v = jnp.var(x, axis=axis, keepdims=True)
    return (x - m) / jnp.sqrt(v + eps)

def _scatter_add(tgt, idx, src, axis=0):
    return tgt.at[idx].add(src)

def _segment_sum(src, seg, n):
    return jax.ops.segment_sum(src, seg, n)
kernel_name = 'mk_seq_preln_d2_jaxref_r4_30180f'

def setup_inputs(seed: int=0):
    np.random.seed(seed)
    _w = jnp.asarray

    def _L0_attn_setup():
        import jax, jax.numpy as jnp
        import numpy as np
        import math
        HIDDEN = 512
        NUM_HEADS = 16
        HEAD_SIZE = HIDDEN // NUM_HEADS
        BATCH = 2
        SEQ = 512
        key = jax.random.key(seed)
        k_x, k_wq, k_bq, k_wo, k_bo = jax.random.split(key, 5)
        scale_in = 1.0 / math.sqrt(HIDDEN)
        return {'x': jax.random.normal(k_x, (BATCH, SEQ, HIDDEN), dtype=jnp.float32), 'Wqkv': jax.random.normal(k_wq, (HIDDEN, 3 * HIDDEN), dtype=jnp.float32) * scale_in, 'bqkv': jax.random.normal(k_bq, (3 * HIDDEN,), dtype=jnp.float32) * 0.01, 'Wo': jax.random.normal(k_wo, (HIDDEN, HIDDEN), dtype=jnp.float32) * scale_in, 'bo': jax.random.normal(k_bo, (HIDDEN,), dtype=jnp.float32) * 0.01}
    _L0_attn_in = _L0_attn_setup()

    def _L0_ffn_setup():
        import jax, jax.numpy as jnp
        import numpy as np
        _FP4_LUT = jnp.array([0.0, 0.5, 1.0, 1.5, 2.0, 3.0, 4.0, 6.0, -0.0, -0.5, -1.0, -1.5, -2.0, -3.0, -4.0, -6.0], dtype=jnp.float32)
        GROUP_SIZE = 128
        EPS = 1e-06

        def _dequant_fp4(packed_i32, scales_f16, group_size):
            out_f, in_p = packed_i32.shape
            w = packed_i32.astype(jnp.uint32)
            shifts = jnp.arange(8, dtype=jnp.uint32) * 4
            nib = w[:, :, None] >> shifts & jnp.uint32(15)
            vals = _FP4_LUT[nib.astype(jnp.int32)].reshape(out_f, in_p * 8)
            s = scales_f16.astype(jnp.float32).T
            s_full = jnp.repeat(s, group_size, axis=1)
            return vals * s_full
        key = jax.random.key(seed)
        k1, k2, k3, k4, k5 = jax.random.split(key, 5)
        B, S, H, I = (4, 512, 512, 1408)
        x = jax.random.normal(k1, (B, S, H), dtype=jnp.float32)
        gate_up_packed = jax.random.randint(k2, (2 * I, H // 8), 0, 2147483647, dtype=jnp.int32)
        gate_up_scales = jax.random.uniform(k3, (H // GROUP_SIZE, 2 * I), dtype=jnp.float32).astype(jnp.float16)
        down_packed = jax.random.randint(k4, (H, I // 8), 0, 2147483647, dtype=jnp.int32)
        down_scales = jax.random.uniform(k5, (I // GROUP_SIZE, H), dtype=jnp.float32).astype(jnp.float16)
        return {'x': x, 'gate_up_packed': gate_up_packed, 'gate_up_scales': gate_up_scales, 'down_packed': down_packed, 'down_scales': down_scales}
    _L0_ffn_in = _L0_ffn_setup()

    def _L1_attn_setup():
        import jax, jax.numpy as jnp
        import numpy as np
        key = jax.random.key(seed)
        k1, k2, k3, k4, k5 = jax.random.split(key, 5)
        B, S, D = (4, 1024, 512)
        x = jax.random.normal(k1, (B, S, D), dtype=jnp.float32)
        W_in = jax.random.normal(k2, (D, D), dtype=jnp.float32) / np.sqrt(D)
        W_out = jax.random.normal(k3, (D, D), dtype=jnp.float32) / np.sqrt(D)
        decay = jax.random.normal(k4, (D,), dtype=jnp.float32) * 0.1
        bias = jax.random.normal(k5, (D,), dtype=jnp.float32) * 0.02
        return {'x': x, 'W_in': W_in, 'W_out': W_out, 'decay': decay, 'bias': bias}
    _L1_attn_in = _L1_attn_setup()

    def _L1_ffn_setup():
        import jax, jax.numpy as jnp
        import numpy as np
        H = 512
        F = 352
        E = 64
        TOP_K = 6
        CAP = 128
        SCALE = 1.0
        F_SH = 2 * F
        B, S = (1, 512)
        key = jax.random.key(seed)
        ks = jax.random.split(key, 8)
        s = 0.02
        return {'hidden_states': jax.random.normal(ks[0], (B, S, H), jnp.float32), 'gate_w': jax.random.normal(ks[1], (E, H), jnp.float32) * s, 'w_gate': jax.random.normal(ks[2], (E, H, F), jnp.float32) * s, 'w_up': jax.random.normal(ks[3], (E, H, F), jnp.float32) * s, 'w_down': jax.random.normal(ks[4], (E, F, H), jnp.float32) * s, 'sh_gate': jax.random.normal(ks[5], (F_SH, H), jnp.float32) * s, 'sh_up': jax.random.normal(ks[6], (F_SH, H), jnp.float32) * s, 'sh_down': jax.random.normal(ks[7], (H, F_SH), jnp.float32) * s}
    _L1_ffn_in = _L1_ffn_setup()
    _d = {'L0_attn_x': _L0_attn_in['x'], 'L0_attn_Wqkv': _L0_attn_in['Wqkv'], 'L0_attn_bqkv': _L0_attn_in['bqkv'], 'L0_attn_Wo': _L0_attn_in['Wo'], 'L0_attn_bo': _L0_attn_in['bo'], 'L0_ffn_gate_up_packed': _L0_ffn_in['gate_up_packed'], 'L0_ffn_gate_up_scales': _L0_ffn_in['gate_up_scales'], 'L0_ffn_down_packed': _L0_ffn_in['down_packed'], 'L0_ffn_down_scales': _L0_ffn_in['down_scales'], 'L1_attn_W_in': _L1_attn_in['W_in'], 'L1_attn_W_out': _L1_attn_in['W_out'], 'L1_attn_decay': _L1_attn_in['decay'], 'L1_attn_bias': _L1_attn_in['bias'], 'L1_ffn_gate_w': _L1_ffn_in['gate_w'], 'L1_ffn_w_gate': _L1_ffn_in['w_gate'], 'L1_ffn_w_up': _L1_ffn_in['w_up'], 'L1_ffn_w_down': _L1_ffn_in['w_down'], 'L1_ffn_sh_gate': _L1_ffn_in['sh_gate'], 'L1_ffn_sh_up': _L1_ffn_in['sh_up'], 'L1_ffn_sh_down': _L1_ffn_in['sh_down']}
    _x0 = _d['L0_attn_x']
    _d['L0_attn_x'] = jax.random.normal(jax.random.fold_in(jax.random.key(seed), 1), (2, 1024, 512), dtype=_x0.dtype)
    del _x0
    return _d

def reference(L0_attn_x, L0_attn_Wqkv, L0_attn_bqkv, L0_attn_Wo, L0_attn_bo, L0_ffn_gate_up_packed, L0_ffn_gate_up_scales, L0_ffn_down_packed, L0_ffn_down_scales, L1_attn_W_in, L1_attn_W_out, L1_attn_decay, L1_attn_bias, L1_ffn_gate_w, L1_ffn_w_gate, L1_ffn_w_up, L1_ffn_w_down, L1_ffn_sh_gate, L1_ffn_sh_up, L1_ffn_sh_down):

    def _L0_attn_ref(x, Wqkv, bqkv, Wo, bo):
        import jax, jax.numpy as jnp
        import numpy as np
        import math
        HIDDEN = 512
        NUM_HEADS = 16
        HEAD_SIZE = HIDDEN // NUM_HEADS
        BATCH = 2
        SEQ = 512
        b, s, _ = x.shape
        kqv = x @ Wqkv + bqkv
        kqv = kqv.reshape(b, s, 3, NUM_HEADS, HEAD_SIZE)
        q = kqv[:, :, 0]
        k = kqv[:, :, 1]
        v = kqv[:, :, 2]
        scores = jnp.einsum('bsnh,btnh->bnst', k, q) / math.sqrt(HEAD_SIZE)
        ones = jnp.ones_like(scores)
        scores = jnp.triu(scores) + -10000.0 * jnp.tril(ones, k=-1)
        attn = jax.nn.softmax(scores, axis=2)
        out = jnp.einsum('bnkq,bknh->bqnh', attn, v)
        out = out.reshape(b, s, NUM_HEADS * HEAD_SIZE)
        return out @ Wo + bo

    def _L0_ffn_ref(x, gate_up_packed, gate_up_scales, down_packed, down_scales):
        import jax, jax.numpy as jnp
        import numpy as np
        _FP4_LUT = jnp.array([0.0, 0.5, 1.0, 1.5, 2.0, 3.0, 4.0, 6.0, -0.0, -0.5, -1.0, -1.5, -2.0, -3.0, -4.0, -6.0], dtype=jnp.float32)
        GROUP_SIZE = 128
        EPS = 1e-06

        def _dequant_fp4(packed_i32, scales_f16, group_size):
            out_f, in_p = packed_i32.shape
            w = packed_i32.astype(jnp.uint32)
            shifts = jnp.arange(8, dtype=jnp.uint32) * 4
            nib = w[:, :, None] >> shifts & jnp.uint32(15)
            vals = _FP4_LUT[nib.astype(jnp.int32)].reshape(out_f, in_p * 8)
            s = scales_f16.astype(jnp.float32).T
            s_full = jnp.repeat(s, group_size, axis=1)
            return vals * s_full
        I = gate_up_packed.shape[0] // 2
        w_gu = _dequant_fp4(gate_up_packed, gate_up_scales, GROUP_SIZE)
        w_down = _dequant_fp4(down_packed, down_scales, GROUP_SIZE)
        gate_up = jnp.einsum('bsh,oh->bso', x, w_gu)
        gate, up = (gate_up[..., :I], gate_up[..., I:])
        h = jax.nn.silu(gate) * up
        y = jnp.einsum('bsi,hi->bsh', h, w_down)
        rms = jnp.sqrt(jnp.mean(y * y, axis=-1, keepdims=True) + EPS)
        return y / rms

    def _L1_attn_ref(x, W_in, W_out, decay, bias):
        import jax, jax.numpy as jnp
        import numpy as np
        d = jax.nn.sigmoid(decay)
        projected = jnp.einsum('bsd,ed->bse', x, W_in)

        def step(state, seg_t):
            state = d * state + (1.0 - d) * seg_t
            return (state, state)
        init = jnp.zeros((x.shape[0], x.shape[2]), dtype=x.dtype)
        _, states = jax.lax.scan(step, init, jnp.swapaxes(projected, 0, 1))
        stacked = jnp.swapaxes(states, 0, 1)
        return jnp.einsum('bsd,ed->bse', stacked, W_out) + bias[None, None, :]

    def _L1_ffn_ref(hidden_states, gate_w, w_gate, w_up, w_down, sh_gate, sh_up, sh_down):
        import jax, jax.numpy as jnp
        import numpy as np
        H = 512
        F = 352
        E = 64
        TOP_K = 6
        CAP = 128
        SCALE = 1.0
        F_SH = 2 * F
        B, S = (1, 512)
        b, s, _ = hidden_states.shape
        x = hidden_states.reshape(-1, H)
        T = x.shape[0]
        logits = x.astype(jnp.float32) @ gate_w.astype(jnp.float32).T
        scores = jax.nn.softmax(logits, axis=-1)
        topk_w, topk_idx = jax.lax.top_k(scores, TOP_K)
        topk_w = topk_w * SCALE
        eid = topk_idx.reshape(-1)
        x_exp = jnp.repeat(x, TOP_K, axis=0)
        order = jnp.argsort(eid)
        eid_s = eid[order]
        counts = jnp.bincount(eid, length=E)
        starts = jnp.cumsum(counts) - counts
        pos = jnp.arange(T * TOP_K) - starts[eid_s]
        valid = pos < CAP
        pos_c = jnp.where(valid, pos, CAP)
        buf = jnp.zeros((E, CAP + 1, H), x.dtype).at[eid_s, pos_c].set(x_exp[order])
        g = jax.nn.silu(jnp.einsum('ech,ehf->ecf', buf, w_gate))
        u = jnp.einsum('ech,ehf->ecf', buf, w_up)
        d = jnp.einsum('ecf,efh->ech', g * u, w_down)
        out_s = jnp.where(valid[:, None], d[eid_s, pos_c], 0.0)
        out_exp = jnp.zeros_like(out_s).at[order].set(out_s)
        y = jnp.einsum('tkh,tk->th', out_exp.reshape(T, TOP_K, H), topk_w)
        y = y.astype(x.dtype).reshape(b, s, H)
        gs = jax.nn.silu(hidden_states @ sh_gate.T)
        us = hidden_states @ sh_up.T
        y = y + gs * us @ sh_down.T
        return y
    x = L0_attn_x
    x = x + _L0_attn_ref(_layernorm(x, axis=-1), L0_attn_Wqkv, L0_attn_bqkv, L0_attn_Wo, L0_attn_bo)
    x = x + _L0_ffn_ref(_layernorm(x, axis=-1), L0_ffn_gate_up_packed, L0_ffn_gate_up_scales, L0_ffn_down_packed, L0_ffn_down_scales)
    x = x + _L1_attn_ref(_layernorm(x, axis=-1), L1_attn_W_in, L1_attn_W_out, L1_attn_decay, L1_attn_bias)
    x = x + _L1_ffn_ref(_layernorm(x, axis=-1), L1_ffn_gate_w, L1_ffn_w_gate, L1_ffn_w_up, L1_ffn_w_down, L1_ffn_sh_gate, L1_ffn_sh_up, L1_ffn_sh_down)
    return x

_drawn_inputs = setup_inputs


def setup_inputs(seed=0):
    import zlib

    import numpy as np

    out = dict(_drawn_inputs(seed))
    spreads = {}
    factors = {'L0_attn_bqkv': 4.407,
     'L0_attn_bo': 4.704,
     'L1_attn_decay': 3.236,
     'L1_attn_bias': 4.471,
     'L1_ffn_gate_w': 8.0,
     'L1_ffn_w_gate': 8.0,
     'L1_ffn_w_up': 8.0,
     'L1_ffn_w_down': 8.0,
     'L1_ffn_sh_gate': 8.0,
     'L1_ffn_sh_up': 8.0,
     'L1_ffn_sh_down': 8.0}
    for name, (base, spread) in spreads.items():
        noise = np.random.default_rng([zlib.crc32(name.encode()), seed]).standard_normal(out[name].shape)
        drawn = base * np.exp(spread * noise) if base else spread * noise
        out[name] = jnp.asarray(drawn.astype(out[name].dtype))
    for name, factor in factors.items():
        out[name] = (out[name] * factor).astype(out[name].dtype)
    return out
```

```python
import concourse.bass as bass
from concourse import mybir

ALU = mybir.AluOpType
ACT = mybir.ActivationFunctionType
AX = mybir.AxisListType
F32 = mybir.dt.float32
F32R = mybir.dt.float32r
BF16 = mybir.dt.bfloat16
F16 = mybir.dt.float16
I32 = mybir.dt.int32
U32 = mybir.dt.uint32

P = 128
B, S, D = 2, 1024, 512
T = B * S
NT = T // P
CH = 512
NCH = T // CH
TPC = CH // P
KT = D // P
H, HD = 16, 32
I0 = 1408
G0 = I0 // P
E, F, CAP, TOPK = 64, 352, 128, 6
FS = 2 * F
LN_EPS = 1e-5
RMS_EPS = 1e-6
XS = D + E
NEG = -1e30


class Memory:
    pass


class Arena:

    def __init__(self, nc, at=0):
        self.nc, self.at = nc, at

    def put(self, name, shape, dtype):
        size = mybir.dt.size(dtype)
        for n in shape[1:]:
            size *= n
        t = self.nc.alloc_sbuf_tensor_at(name, shape, dtype, offset=self.at)
        self.at += (size + 31) // 32 * 32
        return t


def setup_memory(nc, a):
    m = Memory()
    start = (nc.sbuf_base + 31) // 32 * 32
    arena = Arena(nc, start)
    m.x = arena.put("x_residual", [P, NT, D], F32)
    m.ident = arena.put("ident", [P, P], F32)
    m.ident16 = arena.put("ident16", [P, P], BF16)
    m.mask_qk = arena.put("mask_qk", [P, P], BF16)
    m.mask_kq = arena.put("mask_kq", [P, P], BF16)
    m.bqk = arena.put("bqk", [P, 2 * KT], F32)
    m.bv = arena.put("bv_rows", [P, D], F32)
    m.bo = arena.put("bo_rows", [P, D], F32)
    m.b1 = arena.put("b1_rows", [P, D], F32)
    m.stats = arena.put("ln_stats", [P, TPC, 6], F32)
    m.mv = arena.put("ln_mean_var", [P, TPC, 2], F32)
    m.rstd = arena.put("ln_rstd", [P, TPC], F32)
    m.base = arena.at
    m.bank = [nc.alloc_psum_tensor(f"bank{i}", [P, 512], F32) for i in range(8)]
    return m


class InverseRoot:

    STEPS = 3

    def __init__(self, nc, arena, tag, n):
        self.v = arena.put(f"{tag}_root_v", [P, n], F32)
        self.half = arena.put(f"{tag}_root_half", [P, n], I32)
        self.y0 = arena.put(f"{tag}_root_y0", [P, n], I32)
        self.y = arena.put(f"{tag}_root_y", [P, n], F32)
        self.t = arena.put(f"{tag}_root_t", [P, n], F32)
        self.v_ready = nc.alloc_semaphore(f"{tag}_root_v_ready")
        self.half_ready = nc.alloc_semaphore(f"{tag}_root_half_ready")
        self.ready = nc.alloc_semaphore(f"{tag}_root_guess_ready")
        self.step = nc.alloc_semaphore(f"{tag}_root_step")
        self.guesses = self.steps = 0

    def vector_guess(self, dve, src, scale, eps):
        self.guesses += 1
        dve.tensor_scalar(self.v[:, :], src, scale, eps, ALU.mult, ALU.add).then_inc(self.v_ready, 1)
        dve.wait_ge(self.v_ready, self.guesses)
        dve.tensor_scalar(self.half[:, :], self.v[:, :].bitcast(I32), 1, 0, ALU.logical_shift_right,
                          ALU.bitwise_or).then_inc(self.half_ready, 1)
        dve.wait_ge(self.half_ready, self.guesses)
        dve.tensor_scalar(self.y0[:, :], self.half[:, :], -1.0, float(0x5F3759DF), ALU.mult,
                          ALU.add).then_inc(self.ready, 1)

    def gpsimd_refine(self, pool, out, out_ready):
        def then(instruction):
            self.steps += 1
            instruction.then_inc(self.step, 1)
            pool.wait_ge(self.step, self.steps)

        y = self.y0[:, :].bitcast(F32)
        for n in range(self.STEPS):
            then(pool.tensor_tensor(self.t[:, :], y, y, ALU.mult))
            then(pool.tensor_tensor(self.t[:, :], self.t[:, :], self.v[:, :], ALU.mult))
            then(pool.tensor_scalar(self.t[:, :], self.t[:, :], -0.5, 1.5, ALU.mult, ALU.add))
            if n < self.STEPS - 1:
                then(pool.tensor_tensor(self.y[:, :], y, self.t[:, :], ALU.mult))
                y = self.y[:, :]
            else:
                pool.tensor_tensor(out, y, self.t[:, :], ALU.mult).then_inc(out_ready, 1)


class LayerNorm:

    def __init__(self, nc, m, arena, tag, banks=(0, 1), buffers=2, nibbles=False):
        self.nc, self.m, self.banks, self.buffers, self.nibbles = nc, m, banks, buffers, nibbles
        self.xn = arena.put(f"{tag}_xn", [P, TPC, D], F32)
        self.hi = [arena.put(f"{tag}_xt_hi{i}", [P, KT, CH], F32R) for i in range(buffers)]
        self.lo = [arena.put(f"{tag}_xt_lo{i}", [P, KT, CH], F32R) for i in range(buffers)]
        s = lambda name: nc.alloc_semaphore(f"{tag}_{name}")
        self.guess = InverseRoot(nc, arena, tag, TPC)
        self.stats_ready, self.mean_ready = s("stats_ready"), s("mean_ready")
        self.rstd_ready, self.xn_ready = s("rstd_ready"), s("xn_ready")
        self.turned, self.hi_ready, self.lo_ready = s("turned"), s("hi_ready"), s("lo_ready")

    def vector_stats(self, dve, c):
        m = self.m
        if c >= 1:
            dve.wait_ge(self.xn_ready, TPC * c)
        for j in range(TPC):
            dve.bn_stats(m.stats[:, j, :], m.x[:, TPC * c + j, :]).then_inc(self.stats_ready, 1)
        for j in range(TPC):
            dve.wait_ge(self.stats_ready, TPC * c + j + 1)
            dve.bn_aggr(m.mv[:, j, :], m.stats[:, j, :]).then_inc(self.mean_ready, 1)
        dve.wait_ge(self.mean_ready, TPC * (c + 1))
        if c >= 1:
            dve.wait_ge(self.rstd_ready, c)
        self.guess.vector_guess(dve, m.mv[:, :, 1], 1.0, LN_EPS)

    def gpsimd_rstd(self, pool, c):
        pool.wait_ge(self.guess.ready, c + 1)
        self.guess.gpsimd_refine(pool, self.m.rstd[:, :], self.rstd_ready)

    def vector_normalize(self, dve, c):
        m = self.m
        dve.wait_ge(self.rstd_ready, c + 1)
        for j in range(TPC):
            if c >= 1:
                dve.wait_ge(self.turned, TPC * (c - 1) + j + 1)
            out, x = self.xn[:, j, :], m.x[:, TPC * c + j, :]
            if self.nibbles:
                out = out.rearrange("p (k i w) -> p k i w", i=8, w=16)
                x = x.rearrange("p (k w i) -> p k i w", i=8, w=16)
            dve.tensor_scalar(out, x, m.mv[:, j, 0:1], m.rstd[:, j:j + 1],
                              ALU.subtract, ALU.mult).then_inc(self.xn_ready, 1)

    def tensor_turn(self, pe, c, j):
        t = TPC * c + j
        bank = self.m.bank[self.banks[t % 2]]
        pe.wait_ge(self.xn_ready, t + 1)
        if t >= 2:
            pe.wait_ge(self.lo_ready, t - 1)
        for k in range(KT):
            last = pe.transpose(bank[:, k * P:(k + 1) * P], self.xn[:, j, k * P:(k + 1) * P], self.m.ident[:, :])
        last.then_inc(self.turned, 1)

    def scalar_hi(self, act, c, j):
        t = TPC * c + j
        act.wait_ge(self.turned, t + 1)
        src = self.m.bank[self.banks[t % 2]][:, :].rearrange("p (k n) -> p k n", k=KT)
        act.activation(self.hi[c % self.buffers][:, :, j * P:(j + 1) * P], src, ACT.Copy).then_inc(self.hi_ready, 1)

    def vector_lo(self, dve, c, j):
        t = TPC * c + j
        dve.wait_ge(self.hi_ready, t + 1)
        src = self.m.bank[self.banks[t % 2]][:, :].rearrange("p (k n) -> p k n", k=KT)
        b, cols = c % self.buffers, slice(j * P, (j + 1) * P)
        dve.tensor_tensor(self.lo[b][:, :, cols], src, self.hi[b][:, :, cols].bitcast(F32),
                          ALU.subtract).then_inc(self.lo_ready, 1)


def product3(pe, out, terms):
    n = len(terms)
    for i, (sh, sl, mh, ml) in enumerate(terms):
        pe.matmul(out, sh, mh, start=(i == 0), stop=False)
        pe.matmul(out, sh, ml, start=False, stop=False)
        last = pe.matmul(out, sl, mh, start=False, stop=(i == n - 1))
    return last


def qkv_phase(nc, m, a):
    arena = Arena(nc, m.base)
    m.v = arena.put("v_all", [P, B * H, S // P, HD], F32)
    m.after_v = arena.at
    w_raw = arena.put("wqkv_raw", [P, KT, 3 * D], F32)
    w_hi = arena.put("wqkv_hi", [P, KT, 3 * D], F32R)
    w_lo = arena.put("wqkv_lo", [P, KT, 3 * D], F32R)
    ln = LayerNorm(nc, m, arena, "ln1")
    STAGES = 4
    st_hi = [arena.put(f"qk_stage_hi{i}", [P, CH], F32R) for i in range(STAGES)]
    st_lo = [arena.put(f"qk_stage_lo{i}", [P, CH], F32R) for i in range(STAGES)]

    s = nc.alloc_semaphore
    x_loaded = [s(f"x_loaded{c}") for c in range(NCH)]
    w_loaded = [s(f"wqkv_loaded{k}") for k in range(KT)]
    w_hi_ready, w_lo_ready = s("wqkv_hi_ready"), s("wqkv_lo_ready")
    ident_set, consts_ready = s("ident_set"), s("consts_ready")
    bias_loaded = s("bias_loaded")
    product_done, hi_ready, unit_used = s("qkv_product_done"), s("qk_hi_ready"), s("qkv_unit_used")
    stored = [s(f"qk_stored{i}") for i in range(STAGES)]
    UNITS = 2 * KT + TPC
    FIRST, BANKS = 2, 6

    with nc.Block() as block:

        @block.sync
        def _(sp):
            xv = a["x"].rearrange("(t p) d -> p t d", p=P)
            for c in range(NCH):
                sp.dma_start(m.x[:, TPC * c:TPC * (c + 1), :], xv[:, TPC * c:TPC * (c + 1), :]).then_inc(x_loaded[c], 16)
                if c == 0:
                    for k in range(KT):
                        sp.dma_start(w_raw[:, k, :], a["wqkv"][k * P:(k + 1) * P, :]).then_inc(w_loaded[k], 16)
                    with nc.allow_non_contiguous_dma("eight small bias columns"):
                        sp.dma_start(m.bqk[:, :], a["bqkv"][0:2 * D].rearrange("(n p) -> p n", p=P)).then_inc(bias_loaded, 16)
                    sp.dma_start(m.bv[:, :], a["bqkv"][2 * D:3 * D].partition_broadcast(P)).then_inc(bias_loaded, 16)
                    sp.dma_start(m.bo[:, :], a["bo"].partition_broadcast(P)).then_inc(bias_loaded, 16)
                    sp.dma_start(m.b1[:, :], a["b1"].partition_broadcast(P)).then_inc(bias_loaded, 16)
            q = 0
            for c in range(NCH):
                b, col = c // 2, (c % 2) * CH
                for n in range(2 * KT):
                    sp.wait_ge(unit_used, UNITS * c + n + 1)
                    which, o = n // KT, n % KT
                    for half, st in ((0, st_hi), (1, st_lo)):
                        sp.dma_start(a["qk"][which, half, b, o * P:(o + 1) * P, col:col + CH],
                                     st[q % STAGES][:, :].bitcast(F32)).then_inc(stored[q % STAGES], 16)
                    q += 1
            for i in range(STAGES):
                sp.wait_ge(stored[i], 32 * (q // STAGES))

        @block.gpsimd
        def _(pool):
            pool.memset(m.ident[:, :], 0.0).then_inc(ident_set, 1)
            pool.memset(m.ident16[:, :], 0.0).then_inc(ident_set, 1)
            pool.memset(m.mask_qk[:, :], 0.0).then_inc(ident_set, 1)
            pool.memset(m.mask_kq[:, :], 0.0).then_inc(ident_set, 1)
            pool.wait_ge(ident_set, 4)
            for t in (m.ident, m.ident16):
                pool.affine_select(out=t[:, :], in_=t[:, :], compare_op=ALU.not_equal, fill=1.0, base=0,
                                   pattern=[[-1, P]], channel_multiplier=1).then_inc(consts_ready, 1)
            pool.affine_select(out=m.mask_qk[:, :], in_=m.mask_qk[:, :], compare_op=ALU.is_ge, fill=NEG, base=0,
                               pattern=[[-1, P]], channel_multiplier=1).then_inc(consts_ready, 1)
            pool.affine_select(out=m.mask_kq[:, :], in_=m.mask_kq[:, :], compare_op=ALU.is_ge, fill=NEG, base=0,
                               pattern=[[1, P]], channel_multiplier=-1).then_inc(consts_ready, 1)
            for c in range(NCH):
                ln.gpsimd_rstd(pool, c)

        @block.tensor
        def _(pe):
            pe.wait_ge(consts_ready, 4)
            for j in range(TPC):
                ln.tensor_turn(pe, 0, j)
            for c in range(NCH):
                hi, lo = ln.hi[c % 2], ln.lo[c % 2]
                pe.wait_ge(ln.lo_ready, TPC * (c + 1))
                if c == 0:
                    pe.wait_ge(w_lo_ready, KT)
                for n in range(UNITS):
                    u = UNITS * c + n
                    if u >= BANKS:
                        pe.wait_ge(unit_used, u - BANKS + 1)
                    bank = m.bank[FIRST + u % BANKS]
                    if n < 2 * KT:
                        w = slice(n * P, (n + 1) * P)
                        terms = [(w_hi[:, k, w], w_lo[:, k, w], hi[:, k, :], lo[:, k, :]) for k in range(KT)]
                    else:
                        tok = slice((n - 2 * KT) * P, (n - 2 * KT + 1) * P)
                        terms = [(hi[:, k, tok], lo[:, k, tok], w_hi[:, k, 2 * D:], w_lo[:, k, 2 * D:]) for k in range(KT)]
                    product3(pe, bank[:, :], terms).then_inc(product_done, 1)
                    if c + 1 < NCH and n in (5, 6, 7, 8):
                        ln.tensor_turn(pe, c + 1, n - 5)

        @block.scalar
        def _(act):
            for k in range(KT):
                act.wait_ge(w_loaded[k], 16)
                act.activation(w_hi[:, k, :], w_raw[:, k, :], ACT.Copy).then_inc(w_hi_ready, 1)
            for j in range(TPC):
                ln.scalar_hi(act, 0, j)
            act.wait_ge(bias_loaded, 64)
            q = 0
            for c in range(NCH):
                for n in range(UNITS):
                    u = UNITS * c + n
                    if n < 2 * KT:
                        act.wait_ge(product_done, u + 1)
                        if q >= STAGES:
                            act.wait_ge(stored[q % STAGES], 32 * (q // STAGES))
                        act.activation(st_hi[q % STAGES][:, :], m.bank[FIRST + u % BANKS][:, :], ACT.Identity,
                                       bias=m.bqk[:, n:n + 1]).then_inc(hi_ready, 1)
                        q += 1
                    if c + 1 < NCH and n in (5, 6, 7, 8):
                        ln.scalar_hi(act, c + 1, n - 5)

        @block.vector
        def _(dve):
            dve.wait_ge(x_loaded[0], 16)
            ln.vector_stats(dve, 0)
            ln.vector_normalize(dve, 0)
            for j in range(TPC):
                ln.vector_lo(dve, 0, j)
            for k in range(KT):
                dve.wait_ge(w_hi_ready, k + 1)
                dve.tensor_tensor(w_lo[:, k, :], w_raw[:, k, :], w_hi[:, k, :].bitcast(F32),
                                  ALU.subtract).then_inc(w_lo_ready, 1)
            dve.wait_ge(bias_loaded, 64)
            q = 0
            for c in range(NCH):
                if c + 1 < NCH:
                    dve.wait_ge(x_loaded[c + 1], 16)
                    ln.vector_stats(dve, c + 1)
                for n in range(UNITS):
                    u = UNITS * c + n
                    bank = m.bank[FIRST + u % BANKS]
                    if n < 2 * KT:
                        dve.wait_ge(hi_ready, q + 1)
                        dve.scalar_tensor_tensor(out=st_lo[q % STAGES][:, :], in0=bank[:, :], scalar=m.bqk[:, n:n + 1],
                                                 in1=st_hi[q % STAGES][:, :].bitcast(F32), op0=ALU.add,
                                                 op1=ALU.subtract).then_inc(unit_used, 1)
                        q += 1
                    else:
                        dve.wait_ge(product_done, u + 1)
                        b, kt = c // 2, TPC * (c % 2) + n - 2 * KT
                        rows = lambda x: x.rearrange("p (h d) -> p h d", h=H)
                        dve.tensor_tensor(m.v[:, H * b:H * (b + 1), kt, :], rows(bank[:, :]), rows(m.bv[:, :]),
                                          ALU.add).then_inc(unit_used, 1)
                    if c + 1 < NCH:
                        if n == 2:
                            ln.vector_normalize(dve, c + 1)
                        if n in (5, 6, 7, 8):
                            ln.vector_lo(dve, c + 1, n - 5)


def need(engine, semaphore, value):
    if not isinstance(value, int) or value > 0:
        engine.wait_ge(semaphore, value)


def wait_apart(engine, semaphore, value, passed):
    if not isinstance(value, int):
        value = engine.to_reg(value)
    engine.wait_ge(passed, 1)
    need(engine, semaphore, value)


SLICES = 32
GU_COLS, DOWN_COLS = KT * 2 * I0, G0 * D
SLICE = (GU_COLS + DOWN_COLS) // SLICES


class Dequantizer:

    def __init__(self, nc, m, a, arena):
        self.a = a
        put = arena.put
        self.words = [put(f"fp4_words{i}", [P, SLICE], I32) for i in range(2)]
        self.scales = [put(f"fp4_scales{i}", [P, SLICE], F16) for i in range(2)]
        self.bits, self.sign = put("fp4_bits", [P, SLICE], I32), put("fp4_sign", [P, SLICE], I32)
        self.codes, self.bent = put("fp4_codes", [P, SLICE], F32), put("fp4_bent", [P, SLICE], F32)
        self.w = put("fp4_w", [P, SLICE], F32)
        self.hi, self.lo = put("fp4_hi", [P, SLICE], F32R), put("fp4_lo", [P, SLICE], F32)
        self.shift, self.shift3 = put("fp4_shift", [P, 1], I32), put("fp4_shift3", [P, 1], I32)
        s = nc.alloc_semaphore
        self.loaded = [s("fp4_loaded0"), s("fp4_loaded1")]
        self.index_ready, self.shift_ready = s("fp4_index_ready"), s("fp4_shift_ready")
        self.nibbles_ready, self.nibbles_used = s("fp4_nibbles_ready"), s("fp4_nibbles_used")
        self.hi_ready = s("fp4_hi_ready")
        self.step, self.w_ready, self.stored = s("fp4_step"), s("fp4_w_ready"), s("fp4_stored")

    def gpsimd_shifts(self, pool):
        pool.iota(self.shift[:, :], [[0, 1]], base=0, channel_multiplier=1).then_inc(self.index_ready, 1)

    def vector_shifts(self, dve):
        dve.wait_ge(self.index_ready, 1)
        dve.tensor_scalar(self.shift[:, :], self.shift[:, :], 4, 2, ALU.logical_shift_right,
                          ALU.logical_shift_left).then_inc(self.shift_ready, 1)
        dve.wait_ge(self.shift_ready, 1)
        dve.tensor_scalar(self.shift3[:, :], self.shift[:, :], 3.0, None, ALU.add).then_inc(self.shift_ready, 1)

    def sync_load(self, sp, h, u):
        need(sp, self.nibbles_used, h - 1)
        cols, b = bass.ds(h * SLICE, SLICE), u % 2
        sp.dma_start(self.words[b][:, :], self.a["fp4_words"][:, cols]).then_inc(self.loaded[b], 16)
        sp.dma_start(self.scales[b][:, :], self.a["fp4_scales"][cols].partition_broadcast(P)).then_inc(self.loaded[b], 16)

    def vector_nibbles(self, dve, g, u, h):
        if isinstance(h, int) and h == 0:
            dve.wait_ge(self.shift_ready, 2)
        b = u % 2
        dve.wait_ge(self.loaded[b], 32 * (2 * g + u // 2 + 1))
        need(dve, self.nibbles_used, h)
        dve.tensor_scalar(self.bits[:, :], self.words[b][:, :], self.shift[:, :], 7, ALU.logical_shift_right,
                          ALU.bitwise_and).then_inc(self.nibbles_ready, 1)

    def vector_signs(self, dve, u):
        b = u % 2
        dve.tensor_scalar(self.sign[:, :], self.words[b][:, :], self.shift3[:, :], 1, ALU.logical_shift_right,
                          ALU.bitwise_and).then_inc(self.nibbles_ready, 1)

    def vector_codes(self, dve, h):
        dve.wait_ge(self.nibbles_ready, 3 * h + 1)
        dve.scalar_tensor_tensor(out=self.codes[:, :], in0=self.bits[:, :], scalar=4.0, in1=self.bits[:, :],
                                 op0=ALU.max, op1=ALU.add).then_inc(self.nibbles_ready, 1)

    def gpsimd_values(self, pool, h, u):
        STEPS = 4
        done = 0

        def then(instruction):
            nonlocal done
            done += 1
            instruction.then_inc(self.step, 1)
            wait_apart(pool, self.step, h * STEPS + done, self.index_ready)

        wait_apart(pool, self.nibbles_ready, 3 * (h + 1), self.index_ready)
        then(pool.tensor_scalar(self.bent[:, :], self.codes[:, :], 12.0, -16.0, ALU.max, ALU.add))
        then(pool.tensor_tensor(self.codes[:, :], self.codes[:, :], self.bent[:, :], ALU.add))
        then(pool.tensor_scalar(self.bent[:, :], self.sign[:, :], -1.0, 0.5, ALU.mult, ALU.add))
        then(pool.tensor_tensor(self.bent[:, :], self.bent[:, :], self.scales[u % 2][:, :], ALU.mult))
        need(pool, self.stored, 48 * h)
        pool.tensor_tensor(self.w[:, :], self.codes[:, :], self.bent[:, :], ALU.mult).then_inc(self.nibbles_used, 1)

    def scalar_hi(self, act, h):
        act.wait_ge(self.nibbles_used, h + 1)
        need(act, self.stored, 48 * h)
        act.activation(self.hi[:, :], self.w[:, :], ACT.Copy).then_inc(self.hi_ready, 1)

    def vector_lo(self, dve, h):
        dve.wait_ge(self.hi_ready, h + 1)
        dve.tensor_tensor(self.lo[:, :], self.w[:, :], self.hi[:, :].bitcast(F32), ALU.subtract).then_inc(self.w_ready, 1)

    def sync_store(self, sp, h):
        sp.wait_ge(self.w_ready, h + 1)
        cols = bass.ds(h * SLICE, SLICE)
        for n, t in enumerate((self.w, self.hi, self.lo)):
            sp.dma_start(self.a["fp4_out"][n, :, cols], t[:, :].bitcast(F32)).then_inc(self.stored, 16)


def attention_phase(nc, m, a):
    QT = S // P
    HEADS = B * H
    SLOTS = 4
    AHEAD = 2
    ROWS = 3 * HD
    scale = HD ** -0.5
    MAX_UNITS = [(q, half, min(CH, (q + 1) * P - half * CH)) for q in range(QT) for half in range(1 + q // TPC)]
    EXP_UNITS = [(k, max(k * P, c * CH), (c + 1) * CH - max(k * P, c * CH)) for c in range(2) for k in range((c + 1) * TPC)]
    N = len(MAX_UNITS)
    assert N == len(EXP_UNITS) and N % 6 == 0
    LAG = 2
    LAST0 = max(i for i, (k, q0, n) in enumerate(EXP_UNITS) if q0 < CH)
    MAXB, EXPB, OUTB = (0, 1, 7), (2, 3, 4), (5, 6)
    TURNED = (OUTB[0], slice(2 * HD, 2 * HD + 2 * QT))
    EXPS = 6
    PIECES = 8
    NIBBLES_AT = 3
    PIECE_AT = {(SLOTS - 1, 9): 0, (SLOTS - 1, 11): 1, (0, 1): 2, (0, 4): 3, (0, 6): 4, (0, 8): 5, (0, 11): 6, (1, 1): 7}

    arena = Arena(nc, m.after_v)
    m.attn = arena.put("attn_t", [P, HEADS // SLOTS, S], F32)
    wo_raw = Arena(nc, arena.at - 4 * KT * D).put("wo_raw", [P, KT, D], F32)
    wo_hi = arena.put("wo_hi", [P, KT, D], F32R)
    wo_lo = arena.put("wo_lo", [P, KT, D], F32R)
    stacks_at = arena.at
    qs = [arena.put(f"q_stack{i}", [P, S], F32R) for i in range(SLOTS)]
    ks = [arena.put(f"k_stack{i}", [P, S], F32R) for i in range(SLOTS)]
    probs = [arena.put(f"probs{i}", [P, CH], F32) for i in range(EXPS)]
    parts = [arena.put(f"max_parts{i}", [P, 2, QT], F32) for i in range(2)]
    top = arena.put("neg_max", [P, 2, QT], F32)
    top_t = [arena.put(f"neg_max_t{i}", [2 * QT, P], F32R) for i in range(2)]
    vs = [arena.put(f"v_ones{i}", [P, QT, 2 * HD], F32) for i in range(SLOTS)]
    out_t = arena.put("out_t", [P, S], F32)
    sums_t = arena.put("sums_t", [P, S], F32)
    dq = Dequantizer(nc, m, a, arena)
    arena = Arena(nc, stacks_at)
    at_hi = [arena.put(f"attn_t_hi{i}", [P, KT, P], F32R) for i in range(2)]
    at_lo = [arena.put(f"attn_t_lo{i}", [P, KT, P], F32R) for i in range(2)]

    s = nc.alloc_semaphore
    ones_set = s("ones_set")
    stack_loaded = [s(f"stack_loaded{i}") for i in range(SLOTS)]
    max_placed = [s(f"max_placed{i}") for i in range(SLOTS)]
    max_scored, max_part_ready, max_joined = s("max_scored"), s("max_part_ready"), s("max_joined")
    neg_hi_ready, neg_ready = s("neg_max_hi_ready"), s("neg_max_ready")
    max_turned, max_copied = s("max_turned"), s("max_copied")
    scored, exp_ready, weighed = s("scored"), s("exp_ready"), s("weighed")
    v_placed, out_copied = s("v_placed"), s("out_copied")
    inverted, normalized = s("sums_inverted"), s("group_normalized")
    wo_loaded, wo_hi_ready, wo_ready, bias_added = s("wo_loaded"), s("wo_hi_ready"), s("wo_ready"), s("bo_added")
    a_hi, a_lo = s("attn_hi_ready"), s("attn_lo_ready")
    projected, x_added = s("wo_projected"), s("wo_added")

    GROUPS = HEADS // SLOTS

    def over_heads(engine, step):
        for u in range(SLOTS):
            step(0, u, u)
        with engine.Fori(1, GROUPS - 1) as g:
            for u in range(SLOTS):
                step(g, u, g * SLOTS + u)
        for u in range(SLOTS):
            step(GROUPS - 1, u, (GROUPS - 1) * SLOTS + u)

    def is_const(h, low, high=HEADS):
        return isinstance(h, int) and not low <= h < high

    with nc.Block() as block:

        @block.sync
        def _(sp):
            parts_of = a["qk"].rearrange("w l b (h r) t -> w l (b h) r t", r=HD)

            def load(h, u):
                for row, half in enumerate((0, 0, 1)):
                    sp.dma_start(qs[u][row * HD:(row + 1) * HD, :].bitcast(F32),
                                 parts_of[0, half, h]).then_inc(stack_loaded[u], 16)
                for row, half in enumerate((0, 1, 0)):
                    sp.dma_start(ks[u][row * HD:(row + 1) * HD, :].bitcast(F32),
                                 parts_of[1, half, h]).then_inc(stack_loaded[u], 16)

            def place_max(h, u):
                sp.wait_ge(max_copied, h + 1)
                for half in range(2):
                    sp.dma_start(qs[u][ROWS + half:ROWS + half + 1, :].rearrange("a (t c) -> a t c", c=P).bitcast(F32),
                                 top_t[u % 2][half * QT:(half + 1) * QT, :].bitcast(F32)).then_inc(max_placed[u], 16)

            def step(g, u, h):
                if not is_const(h, 1, HEADS - SLOTS + 1):
                    sp.wait_ge(scored, N * h)
                    load(h - 1 + SLOTS, (u - 1) % SLOTS)
                if not is_const(h, 1, HEADS - 1):
                    place_max(h + 1, (u + 1) % SLOTS)
                if not is_const(h, 0, HEADS - 1):
                    dq.sync_load(sp, h + 1, u + 1)
                if not is_const(h, 1):
                    dq.sync_store(sp, h - 1)

            for u in range(SLOTS):
                load(u, u)
            sp.dma_start(wo_raw[:, :, :], a["wo"].rearrange("(k p) n -> p k n", p=P)).then_inc(wo_loaded, 16)
            dq.sync_load(sp, 0, 0)
            for u in range(AHEAD):
                place_max(u, u)
            over_heads(sp, step)
            dq.sync_store(sp, HEADS - 1)
            sp.wait_ge(dq.stored, 48 * HEADS)

        @block.gpsimd
        def _(pool):
            for i in range(SLOTS):
                pool.memset(ks[i][ROWS:ROWS + 2, :].bitcast(F32), 1.0).then_inc(ones_set, 1)
            pool.wait_ge(ones_set, SLOTS)
            for i in range(SLOTS):
                pool.memset(vs[i][:, :, HD:], 1.0).then_inc(ones_set, 1)
            pool.wait_ge(ones_set, 2 * SLOTS)
            dq.gpsimd_shifts(pool)

            def place_v(h, u):
                pool.tensor_copy(vs[u % SLOTS][:, :, 0:HD], m.v[:, h, :, :]).then_inc(v_placed, 1)

            def step(g, u, h):
                if not is_const(h, 0, HEADS - AHEAD):
                    need(pool, weighed, N * (h + AHEAD - SLOTS + 1))
                    place_v(h + AHEAD, u + AHEAD)
                dq.gpsimd_values(pool, h, u)
                if isinstance(h, int) and h >= HEADS - SLOTS:
                    for t in range(u * NT // SLOTS, (u + 1) * NT // SLOTS):
                        pool.tensor_tensor(m.x[:, t, :], m.x[:, t, :], m.bo[:, :], ALU.add).then_inc(bias_added, 1)

            for u in range(AHEAD):
                place_v(u, u)
            pool.wait_ge(wo_loaded, 16)
            pool.tensor_copy(wo_hi[:, :, :], wo_raw[:, :, :]).then_inc(wo_hi_ready, 1)
            pool.wait_ge(wo_hi_ready, 1)
            pool.tensor_tensor(wo_lo[:, :, :], wo_raw[:, :, :], wo_hi[:, :, :].bitcast(F32),
                               ALU.subtract).then_inc(wo_ready, 1)
            over_heads(pool, step)

        @block.tensor
        def _(pe):
            def max_unit(h, u, i):
                q, half, n = MAX_UNITS[i]
                need(pe, max_part_ready, N * h + i - 2)
                bank = m.bank[MAXB[i % 3]]
                diagonal = (q + 1) * P - half * CH == n
                last = pe.matmul(bank[:, 0:n], qs[u][0:ROWS, q * P:(q + 1) * P], ks[u][0:ROWS, half * CH:half * CH + n],
                                 start=True, stop=not diagonal)
                if diagonal:
                    last = pe.matmul(bank[:, n - P:n], m.ident16[:, :], m.mask_qk[:, :], start=False, stop=True)
                last.then_inc(max_scored, 1)

            def exp_unit(h, u, i):
                k, q0, n = EXP_UNITS[i]
                need(pe, exp_ready, N * h + i - 2)
                bank = m.bank[EXPB[i % 3]]
                diagonal = q0 == k * P
                last = pe.matmul(bank[:, 0:n], ks[u][0:ROWS + 2, k * P:(k + 1) * P], qs[u][0:ROWS + 2, q0:q0 + n],
                                 start=True, stop=not diagonal)
                if diagonal:
                    last = pe.matmul(bank[:, 0:P], m.ident16[:, :], m.mask_kq[:, :], start=False, stop=True)
                last.then_inc(scored, 1)

            def value_unit(h, u, i):
                k, q0, n = EXP_UNITS[i]
                c = q0 // CH
                if i == 0:
                    pe.wait_ge(v_placed, h + 1)
                if k == 0:
                    need(pe, out_copied, 4 * h - 2 + 2 * c)
                pe.wait_ge(exp_ready, N * h + i + 1)
                pe.matmul(m.bank[OUTB[c]][0:2 * HD, q0 - c * CH:q0 - c * CH + n], vs[u][:, k, :], probs[i % EXPS][:, 0:n],
                          start=(k == 0), stop=(k == (c + 1) * TPC - 1)).then_inc(weighed, 1)

            def turn_max(h):
                pe.wait_ge(neg_ready, h + 1)
                need(pe, max_copied, h)
                pe.matmul(m.bank[TURNED[0]][TURNED[1], 0:P], top[:, :, :].rearrange("p a q -> p (a q)"), m.ident[:, :],
                          start=True, stop=True).then_inc(max_turned, 1)

            def step(g, u, h):
                ahead = (u + AHEAD) % SLOTS
                for i in range(N):
                    if not is_const(h, 0, HEADS - AHEAD):
                        if i == 0:
                            pe.wait_ge(stack_loaded[ahead], 96 * (g + 1 + (u + AHEAD) // SLOTS))
                        max_unit(h + AHEAD, ahead, i)
                    if i == 0:
                        pe.wait_ge(max_placed[u], 32 * (g + 1))
                    exp_unit(h, u, i)
                    if i >= LAG:
                        value_unit(h, u, i - LAG)
                    elif not is_const(h, 1):
                        value_unit(h - 1, (u - 1) % SLOTS, N - LAG + i)
                    if i == 3 and not is_const(h, 1, HEADS - 1):
                        turn_max(h + 1)

            pe.wait_ge(ones_set, 2 * SLOTS)
            for u in range(AHEAD):
                pe.wait_ge(stack_loaded[u], 96)
                for i in range(N):
                    max_unit(u, u, i)
                turn_max(u)
            over_heads(pe, step)
            for i in range(N - LAG, N):
                value_unit(HEADS - 1, SLOTS - 1, i)

            pe.wait_ge(wo_ready, 1)
            for t in range(NT):
                pe.wait_ge(a_lo, t + 1)
                need(pe, x_added, t - 2)
                product3(pe, m.bank[EXPB[t % 3]][:, :],
                         [(at_hi[t % 2][:, k, :], at_lo[t % 2][:, k, :], wo_hi[:, k, :], wo_lo[:, k, :])
                          for k in range(KT)]).then_inc(projected, 1)

        @block.scalar
        def _(act):
            def copy_max(h, u):
                act.wait_ge(max_turned, h + 1)
                act.activation(top_t[u % 2][:, :], m.bank[TURNED[0]][TURNED[1], 0:P], ACT.Copy).then_inc(max_copied, 1)

            def copy_out(g, u, h, c):
                act.wait_ge(weighed, N * h + (N if c else LAST0 + 1))
                if u == 0:
                    need(act, normalized, PIECES * g - (0 if c else PIECES // 2))
                rows, cols = slice(u * HD, (u + 1) * HD), slice(c * CH, (c + 1) * CH)
                act.activation(out_t[rows, cols], m.bank[OUTB[c]][0:HD, :], ACT.Copy).then_inc(out_copied, 1)
                act.activation(sums_t[rows, cols], m.bank[OUTB[c]][HD:2 * HD, :], ACT.Copy).then_inc(out_copied, 1)

            def step(g, u, h):
                for i in range(N):
                    if i == LAST0 + LAG + 2:
                        copy_out(g, u, h, 0)
                    if i == 3 and not is_const(h, 1):
                        copy_out(*((g, u - 1) if u else (g - 1, SLOTS - 1)), h - 1, 1)
                    if i == 5 and not is_const(h, 1):
                        dq.scalar_hi(act, h - 1)
                    k, q0, n = EXP_UNITS[i]
                    act.wait_ge(scored, N * h + i + 1)
                    need(act, weighed, N * h + i - EXPS + 1)
                    act.activation(probs[i % EXPS][:, 0:n], m.bank[EXPB[i % 3]][:, 0:n], ACT.Exp,
                                   scale=scale).then_inc(exp_ready, 1)
                    if i == 4 and not is_const(h, 1, HEADS - 1):
                        act.wait_ge(max_placed[(u - 1) % SLOTS], 32 * (g + (1 if u else 0)))
                        copy_max(h + 1, u + 1)

            for u in range(AHEAD):
                copy_max(u, u)
            over_heads(act, step)
            for t in range(NT):
                if t == 2:
                    copy_out(GROUPS - 1, SLOTS - 1, HEADS - 1, 1)
                    dq.scalar_hi(act, HEADS - 1)
                b, q = t // QT, t % QT
                act.wait_ge(normalized, PIECES * (b + 1) * KT)
                need(act, projected, t - 1)
                act.activation(at_hi[t % 2][:, :, :], m.attn[:, b * KT:(b + 1) * KT, q * P:(q + 1) * P],
                               ACT.Copy).then_inc(a_hi, 1)

        @block.vector
        def _(dve):
            def max_part(h, u, i):
                q, half, n = MAX_UNITS[i]
                dve.wait_ge(max_scored, N * h + i + 1)
                dve.tensor_reduce(parts[u % 2][:, half, q:q + 1], m.bank[MAXB[i % 3]][:, 0:n], AX.X,
                                  ALU.max).then_inc(max_part_ready, 1)

            def join_max(h, u):
                both = parts[u % 2]
                dve.wait_ge(max_part_ready, N * (h + 1))
                dve.tensor_tensor(both[:, 0, TPC:], both[:, 0, TPC:], both[:, 1, TPC:], ALU.max).then_inc(max_joined, 1)
                need(dve, max_turned, h)
                dve.wait_ge(max_joined, h + 1)
                dve.tensor_scalar(top[:, 0, :].bitcast(F32R), both[:, 0, :], -1.0, None, ALU.mult).then_inc(neg_hi_ready, 1)
                dve.wait_ge(neg_hi_ready, h + 1)
                dve.scalar_tensor_tensor(out=top[:, 1, :].bitcast(F32R), in0=both[:, 0, :], scalar=-1.0, in1=top[:, 0, :],
                                         op0=ALU.mult, op1=ALU.subtract).then_inc(neg_ready, 1)

            def normalize(g, piece):
                cols = slice(piece * S // PIECES, (piece + 1) * S // PIECES)
                if piece == 0:
                    dve.wait_ge(out_copied, 4 * SLOTS * (g + 1) - 2)
                if piece == PIECES // 2:
                    dve.wait_ge(out_copied, 4 * SLOTS * (g + 1))
                dve.reciprocal(sums_t[:, cols], sums_t[:, cols]).then_inc(inverted, 1)
                dve.wait_ge(inverted, PIECES * g + piece + 1)
                dve.tensor_tensor(m.attn[:, g, cols], out_t[:, cols], sums_t[:, cols], ALU.mult).then_inc(normalized, 1)

            def step(g, u, h):
                for i in range(N):
                    if not is_const(h, 0, HEADS - AHEAD):
                        max_part(h + AHEAD, u, i)
                    if (u, i) in PIECE_AT and not is_const(h, SLOTS - 1):
                        normalize(g if u == SLOTS - 1 else g - 1, PIECE_AT[u, i])
                    if i == 7 and not is_const(h, 1):
                        dq.vector_lo(dve, h - 1)
                    if i == NIBBLES_AT:
                        dq.vector_nibbles(dve, g, u, h)
                    if i == NIBBLES_AT + 1:
                        dq.vector_signs(dve, u)
                    if i == NIBBLES_AT + 2:
                        dq.vector_codes(dve, h)
                if not is_const(h, 0, HEADS - AHEAD):
                    join_max(h + AHEAD, u)

            dq.vector_shifts(dve)
            for u in range(AHEAD):
                for i in range(N):
                    max_part(u, u, i)
                join_max(u, u)
            over_heads(dve, step)
            def split_attn(t):
                dve.wait_ge(a_hi, t + 1)
                b, q = t // QT, t % QT
                dve.tensor_tensor(at_lo[t % 2][:, :, :], m.attn[:, b * KT:(b + 1) * KT, q * P:(q + 1) * P],
                                  at_hi[t % 2][:, :, :].bitcast(F32), ALU.subtract).then_inc(a_lo, 1)

            for t in range(2):
                split_attn(t)
            for piece in range(2, PIECES):
                normalize(GROUPS - 1, piece)
            dq.vector_lo(dve, HEADS - 1)
            dve.wait_ge(bias_added, NT)
            for t in range(NT):
                dve.wait_ge(projected, t + 1)
                dve.tensor_tensor(m.x[:, t, :], m.x[:, t, :], m.bank[EXPB[t % 3]][:, :],
                                  ALU.add).then_inc(x_added, 1)
                if t + 2 < NT:
                    split_attn(t + 2)


def ffn_phase(nc, m, a):
    arena = Arena(nc, m.base)
    gu_hi = arena.put("gu_hi", [P, KT, 2 * I0], F32R)
    gu_lo = arena.put("gu_lo", [P, KT, 2 * I0], F32R)
    down = arena.put("down", [P, G0, D], F32)
    ln = LayerNorm(nc, m, arena, "ln2", buffers=1, nibbles=True)
    hidden = arena.put("hidden", [P, G0, CH], F32)
    silu = [arena.put(f"silu{i}", [P, CH], F32) for i in range(2)]
    square = arena.put("y_square", [P, D], F32)
    square_sum = arena.put("y_square_sum", [P, 2], F32)
    y_rms = arena.put("y_inverse_rms", [P, 2], F32)
    root = InverseRoot(nc, arena, "rms", 1)
    GATEB, UPB, DOWNB = (2, 3), (4, 5), (6, 7)

    s = nc.alloc_semaphore
    gate_loaded = [s(f"gate_loaded{k}") for k in range(KT)]
    up_loaded = [s(f"up_loaded{k}") for k in range(KT)]
    down_loaded = s("down_loaded")
    gate_done, up_done = s("gate_done"), s("up_done")
    silu_ready, hidden_ready = s("silu_ready"), s("hidden_ready")
    y_done, squared, rms_ready, y_added = s("y_done"), s("y_squared"), s("rms_ready"), s("y_added")

    with nc.Block() as block:

        @block.sync
        def _(sp):
            for half, loaded in ((0, gate_loaded), (1, up_loaded)):
                for k in range(KT):
                    cols = slice(half * I0, (half + 1) * I0)
                    src = slice(k * 2 * I0 + half * I0, k * 2 * I0 + (half + 1) * I0)
                    for n, w in ((1, gu_hi), (2, gu_lo)):
                        sp.dma_start(w[:, k, cols].bitcast(F32), a["fp4_out"][n, :, src]).then_inc(loaded[k], 16)
            sp.dma_start(down[:, :, :].rearrange("p g n -> p (g n)"), a["fp4_out"][0, :, GU_COLS:]).then_inc(down_loaded, 16)

        @block.gpsimd
        def _(pool):
            for c in range(NCH):
                if c == 0:
                    ln.gpsimd_rstd(pool, c)
                for j in range(TPC):
                    if c + 1 < NCH and j == 0:
                        ln.gpsimd_rstd(pool, c + 1)
                    t = TPC * c + j
                    pool.wait_ge(root.ready, t + 1)
                    need(pool, y_added, t - 1)
                    root.gpsimd_refine(pool, y_rms[:, t % 2:t % 2 + 1], rms_ready)

        @block.tensor
        def _(pe):
            for j in range(TPC):
                ln.tensor_turn(pe, 0, j)
            for c in range(NCH):
                pe.wait_ge(ln.lo_ready, TPC * (c + 1))
                hi, lo = ln.hi[0], ln.lo[0]
                for g in range(G0):
                    n = G0 * c + g
                    need(pe, hidden_ready, n - 1)
                    for half, bank, loaded, done in ((0, GATEB, gate_loaded, gate_done), (1, UPB, up_loaded, up_done)):
                        if c == 0 and g == 0:
                            for k in range(KT):
                                pe.wait_ge(loaded[k], 32)
                        w = slice(half * I0 + g * P, half * I0 + (g + 1) * P)
                        product3(pe, m.bank[bank[n % 2]][:, :],
                                 [(gu_hi[:, k, w], gu_lo[:, k, w], hi[:, k, :], lo[:, k, :])
                                  for k in range(KT)]).then_inc(done, 1)
                if c == 0:
                    pe.wait_ge(down_loaded, 16)
                for j in range(TPC):
                    if c + 1 < NCH:
                        ln.tensor_turn(pe, c + 1, j)
                    t = TPC * c + j
                    if j == 0:
                        pe.wait_ge(hidden_ready, G0 * (c + 1))
                    need(pe, y_added, t - 1)
                    for g in range(G0):
                        last = pe.matmul(m.bank[DOWNB[t % 2]][:, :], hidden[:, g, j * P:(j + 1) * P], down[:, g, :],
                                         start=(g == 0), stop=(g == G0 - 1))
                    last.then_inc(y_done, 1)

        @block.scalar
        def _(act):
            for j in range(TPC):
                ln.scalar_hi(act, 0, j)
            for c in range(NCH):
                for g in range(G0):
                    n = G0 * c + g
                    act.wait_ge(gate_done, n + 1)
                    need(act, hidden_ready, n - 1)
                    act.activation(silu[n % 2][:, :], m.bank[GATEB[n % 2]][:, :], ACT.Silu).then_inc(silu_ready, 1)
                act.wait_ge(up_done, G0 * (c + 1))
                for j in range(TPC):
                    if c + 1 < NCH:
                        ln.scalar_hi(act, c + 1, j)
                    t = TPC * c + j
                    act.wait_ge(y_done, t + 1)
                    need(act, root.v_ready, t - 1)
                    need(act, squared, t)
                    act.activation(square[:, :], m.bank[DOWNB[t % 2]][:, :], ACT.Square,
                                   accum_out=square_sum[:, t % 2:t % 2 + 1]).then_inc(squared, 1)

        @block.vector
        def _(dve):
            def add_y(t):
                dve.wait_ge(rms_ready, t + 1)
                dve.scalar_tensor_tensor(out=m.x[:, t, :], in0=m.bank[DOWNB[t % 2]][:, :], scalar=y_rms[:, t % 2:t % 2 + 1],
                                         in1=m.x[:, t, :], op0=ALU.mult, op1=ALU.add).then_inc(y_added, 1)

            ln.vector_stats(dve, 0)
            ln.vector_normalize(dve, 0)
            for j in range(TPC):
                ln.vector_lo(dve, 0, j)
            for c in range(NCH):
                for g in range(G0):
                    n = G0 * c + g
                    if c + 1 < NCH and g == 4:
                        ln.vector_stats(dve, c + 1)
                    if c + 1 < NCH and g == 7:
                        ln.vector_normalize(dve, c + 1)
                    if g == 0 and c >= 1:
                        dve.wait_ge(y_done, TPC * c)
                    dve.wait_ge(silu_ready, n + 1)
                    dve.wait_ge(up_done, n + 1)
                    dve.tensor_tensor(hidden[:, g, :], silu[n % 2][:, :], m.bank[UPB[n % 2]][:, :],
                                      ALU.mult).then_inc(hidden_ready, 1)
                for j in range(TPC):
                    if c + 1 < NCH:
                        ln.vector_lo(dve, c + 1, j)
                    if j >= 1:
                        add_y(TPC * c + j - 1)
                    t = TPC * c + j
                    dve.wait_ge(squared, t + 1)
                    need(dve, rms_ready, t)
                    root.vector_guess(dve, square_sum[:, t % 2:t % 2 + 1], 1.0 / D, RMS_EPS)
                add_y(TPC * (c + 1) - 1)


def recurrence_phase(nc, m, a):
    arena = Arena(nc, m.base)
    parts = {}
    for name in ("w_in", "w_out"):
        parts[name] = [arena.put(f"{name}_{p}", [P, KT, D], dt) for p, dt in (("raw", F32), ("hi", F32R), ("lo", F32R))]
    ln = LayerNorm(nc, m, arena, "ln3")
    decay = arena.put("decay_cols", [P, 4, KT], F32)
    drive = [arena.put(f"drive{i}", [P, CH], F32) for i in range(2)]
    state = [arena.put(f"state{i}", [P, KT, CH], F32) for i in range(2)]
    st_hi = [arena.put(f"state_hi{i}", [P, KT, CH], F32R) for i in range(2)]
    st_lo = [arena.put(f"state_lo{i}", [P, KT, CH], F32R) for i in range(2)]
    INB, OUTB = (2, 3, 4), (5, 6, 7)

    s = nc.alloc_semaphore
    w_loaded = {n: s(f"{n}_loaded") for n in parts}
    w_hi_ready = {n: s(f"{n}_hi_ready") for n in parts}
    w_ready = {n: s(f"{n}_ready") for n in parts}
    decay_loaded, decay_step = s("decay_loaded"), s("decay_step")
    in_done, drive_ready, scanned = s("in_done"), s("drive_ready"), s("scanned")
    st_hi_ready, st_lo_ready = s("state_hi_ready"), s("state_lo_ready")
    bias_added, out_done, x_added = s("b1_added"), s("out_done"), s("rec_added")

    with nc.Block() as block:

        @block.sync
        def _(sp):
            with nc.allow_non_contiguous_dma("four small decay columns"):
                sp.dma_start(decay[:, 0, :], a["decay"].rearrange("(k p) -> p k", p=P)).then_inc(decay_loaded, 16)
            for name in parts:
                sp.dma_start(parts[name][0][:, :, :], a[name].rearrange("(k p) n -> p k n", p=P)).then_inc(w_loaded[name], 16)

        @block.gpsimd
        def _(pool):
            for c in range(NCH):
                ln.gpsimd_rstd(pool, c)
                pool.wait_ge(ln.xn_ready, TPC * (c + 1))
                for t in range(TPC * c, TPC * (c + 1)):
                    pool.tensor_tensor(m.x[:, t, :], m.x[:, t, :], m.b1[:, :], ALU.add).then_inc(bias_added, 1)

        @block.tensor
        def _(pe):
            def project_in(c):
                hi, lo = ln.hi[c % 2], ln.lo[c % 2]
                pe.wait_ge(ln.lo_ready, TPC * (c + 1))
                for e in range(KT):
                    n = KT * c + e
                    need(pe, drive_ready, n - 2)
                    w = slice(e * P, (e + 1) * P)
                    _, w_hi, w_lo = parts["w_in"]
                    product3(pe, m.bank[INB[n % 3]][:, :],
                             [(w_hi[:, k, w], w_lo[:, k, w], hi[:, k, :], lo[:, k, :]) for k in range(KT)]).then_inc(in_done, 1)
                    if c + 1 < NCH:
                        ln.tensor_turn(pe, c + 1, e)

            for j in range(TPC):
                ln.tensor_turn(pe, 0, j)
            pe.wait_ge(w_ready["w_in"], 1)
            project_in(0)
            pe.wait_ge(w_ready["w_out"], 1)
            for c in range(NCH):
                if c + 1 < NCH:
                    project_in(c + 1)
                pe.wait_ge(st_lo_ready, KT * (c + 1))
                for j in range(TPC):
                    t = TPC * c + j
                    need(pe, x_added, t - 2)
                    tok = slice(j * P, (j + 1) * P)
                    _, w_hi, w_lo = parts["w_out"]
                    product3(pe, m.bank[OUTB[t % 3]][:, :],
                             [(st_hi[c % 2][:, k, tok], st_lo[c % 2][:, k, tok], w_hi[:, k, :], w_lo[:, k, :]) for k in range(KT)]).then_inc(out_done, 1)

        @block.scalar
        def _(act):
            act.wait_ge(decay_loaded, 16)
            act.activation(decay[:, 1, :], decay[:, 0, :], ACT.Exp, scale=-1.0).then_inc(decay_step, 1)
            for name in parts:
                raw, hi, _ = parts[name]
                act.wait_ge(w_loaded[name], 16)
                act.activation(hi[:, :, :], raw[:, :, :], ACT.Copy).then_inc(w_hi_ready[name], 1)
            for j in range(TPC):
                ln.scalar_hi(act, 0, j)
            act.wait_ge(decay_step, 4)
            for c in range(NCH):
                for e in range(KT):
                    n = KT * c + e
                    act.wait_ge(in_done, n + 1)
                    need(act, scanned, n - 1)
                    act.activation(drive[n % 2][:, :], m.bank[INB[n % 3]][:, :], ACT.Copy,
                                   scale=decay[:, 3, e:e + 1]).then_inc(drive_ready, 1)
                    if c + 1 < NCH:
                        ln.scalar_hi(act, c + 1, e)
                    act.wait_ge(scanned, n + 1)
                    if c >= 2 and e == 0:
                        act.wait_ge(out_done, TPC * (c - 1))
                    act.activation(st_hi[c % 2][:, e, :], state[c % 2][:, e, :], ACT.Copy).then_inc(st_hi_ready, 1)

        @block.vector
        def _(dve):
            ln.vector_stats(dve, 0)
            ln.vector_normalize(dve, 0)
            dve.wait_ge(decay_step, 1)
            dve.tensor_scalar(decay[:, 1, :], decay[:, 1, :], 1.0, None, ALU.add).then_inc(decay_step, 1)
            dve.wait_ge(decay_step, 2)
            dve.reciprocal(decay[:, 2, :], decay[:, 1, :]).then_inc(decay_step, 1)
            dve.wait_ge(decay_step, 3)
            dve.tensor_scalar(decay[:, 3, :], decay[:, 2, :], -1.0, 1.0, ALU.mult, ALU.add).then_inc(decay_step, 1)
            for name in parts:
                raw, hi, lo = parts[name]
                dve.wait_ge(w_hi_ready[name], 1)
                dve.tensor_tensor(lo[:, :, :], raw[:, :, :], hi[:, :, :].bitcast(F32), ALU.subtract).then_inc(w_ready[name], 1)
                if name == "w_in":
                    for j in range(TPC):
                        ln.vector_lo(dve, 0, j)

            def add_out(t):
                dve.wait_ge(out_done, t + 1)
                dve.tensor_tensor(m.x[:, t, :], m.x[:, t, :], m.bank[OUTB[t % 3]][:, :], ALU.add).then_inc(x_added, 1)

            for c in range(NCH):
                if c + 1 < NCH:
                    ln.vector_stats(dve, c + 1)
                    ln.vector_normalize(dve, c + 1)
                for e in range(KT):
                    n = KT * c + e
                    dve.wait_ge(drive_ready, n + 1)
                    carry = 0.0 if c % (S // CH) == 0 else state[(c - 1) % 2][:, e, CH - 1:CH]
                    dve.tensor_tensor_scan(state[c % 2][:, e, :], decay[:, 2, e:e + 1].to_broadcast([P, CH]),
                                           drive[n % 2][:, :], carry, ALU.mult, ALU.add).then_inc(scanned, 1)
                    if c + 1 < NCH:
                        ln.vector_lo(dve, c + 1, e)
                    dve.wait_ge(st_hi_ready, n + 1)
                    dve.tensor_tensor(st_lo[c % 2][:, e, :], state[c % 2][:, e, :], st_hi[c % 2][:, e, :].bitcast(F32),
                                      ALU.subtract).then_inc(st_lo_ready, 1)
                if c >= 1:
                    dve.wait_ge(bias_added, TPC * c)
                    for j in range(TPC):
                        add_out(TPC * (c - 1) + j)
            dve.wait_ge(bias_added, NT)
            for t in range(NT - TPC, NT):
                add_out(t)


def router_phase(nc, m, a):
    arena = Arena(nc, m.base)
    m.slot_rows = arena.put("slot_rows", [P, E], U32)
    m.after_slots = arena.at
    GS = (FS + P - 1) // P
    rows = [min(P, FS - g * P) for g in range(GS)]
    w_hi = {n: arena.put(f"{n}_hi", [P, KT, FS], F32R) for n in ("sh_gate", "sh_up")}
    w_lo = {n: arena.put(f"{n}_lo", [P, KT, FS], F32R) for n in ("sh_gate", "sh_up")}
    w_raw = arena.put("sh_up_raw", [P, KT, FS], F32)
    gw_raw = arena.put("gate_w_raw", [P, KT, E], F32)
    gw_hi = arena.put("gate_w_hi", [P, KT, E], F32R)
    gw_lo = arena.put("gate_w_lo", [P, KT, E], F32R)
    down = arena.put("sh_down", [P, GS, D], F32)
    ln = LayerNorm(nc, m, arena, "ln4", buffers=1)
    hidden = arena.put("sh_hidden", [P, GS, CH], F32)
    silu = [arena.put(f"sh_silu{i}", [P, CH], F32) for i in range(2)]
    logits_e = arena.put("logits_e", [E, CH], F32)
    logits = arena.put("logits", [P, TPC, E], F32)
    top = arena.put("logit_max", [P, TPC], F32)
    total = arena.put("exp_sum", [P, TPC], F32)
    scores = arena.put("scores", [P, TPC, E + 2], F32)
    best = arena.put("best", [P, TPC, 8], F32)
    marked = arena.put("marked", [P, TPC, E + 2], F32)
    keys = arena.put("keys", [P, TPC, E], F32)
    ranks = [arena.put(f"ranks{i}", [E, CAP + CH], F32) for i in range(2)]
    kept = arena.put("kept", [E, CAP], F32)
    iota_i = arena.put("key_iota", [P, NT], I32)
    key_of = arena.put("key_of_token", [P, NT], F32)
    slot_i = arena.put("slot_iota", [P, 1], I32)
    slot_f = arena.put("slot_number", [P, 1], F32)
    empty = arena.put("slot_empty", [P, E], F32)
    rows_f = arena.put("slot_rows_f", [P, E], F32)
    zero = arena.put("zero_rows", [P, XS], F32)
    GATEB, UPB, DOWNB = (2, 3), (4, 5), (6, 7)
    EB, TB = DOWNB
    SENTINEL = 2.0
    ROUNDS = CAP // 8

    s = nc.alloc_semaphore
    w_loaded = {n: s(f"{n}_loaded") for n in ("gate_w", "sh_gate", "sh_up", "sh_down")}
    w_hi_ready = {n: s(f"{n}_hi_ready") for n in ("gate_w", "sh_gate", "sh_up")}
    w_ready = {n: s(f"{n}_ready") for n in ("gate_w", "sh_gate", "sh_up")}
    iota_set, zero_set, consts = s("router_iota_set"), s("zero_rows_set"), s("router_consts_ready")
    xn_stored, scores_stored, out_stored = s("xn_stored"), s("scores_stored"), s("out_stored")
    logits_done, logits_copied, logits_turned = s("logits_done"), s("logits_copied"), s("logits_turned")
    max_ready, shifted, exp_ready, sum_ready = s("logit_max_ready"), s("logits_shifted"), s("router_exp_ready"), s("exp_sum_ready")
    inverse_ready, scores_ready = s("exp_inverse_ready"), s("scores_ready")
    best_ready, best_set, marks_ready, keys_ready = s("best_ready"), s("best_set"), s("marks_ready"), s("keys_ready")
    keys_turned, keys_copied, rank_step, kept_moved = s("keys_turned"), s("keys_copied"), s("rank_step"), s("kept_moved")
    kept_turned, empty_ready, rows_ready, slots_ready = s("kept_turned"), s("slot_empty_ready"), s("slot_rows_f_ready"), s("slots_ready")
    gate_done, up_done, silu_ready, hidden_ready = s("sh_gate_done"), s("sh_up_done"), s("sh_silu_ready"), s("sh_hidden_ready")
    y_done, y_added = s("sh_y_done"), s("sh_y_added")
    gate_raw = hidden[:, :, :].rearrange("p g n -> p (g n)")[:, 0:KT * FS].rearrange("p (k n) -> p k n", k=KT)
    raws = {"gate_w": gw_raw[:, :, :], "sh_gate": gate_raw, "sh_up": w_raw[:, :, :]}
    parts = {"gate_w": (gw_hi, gw_lo), "sh_gate": (w_hi["sh_gate"], w_lo["sh_gate"]), "sh_up": (w_hi["sh_up"], w_lo["sh_up"])}
    xn_rows = a["xs"][0:T, 0:D].rearrange("(t p) d -> p t d", p=P)
    score_rows = a["xs"][0:T, D:XS].rearrange("(t p) e -> p t e", p=P)
    out_rows = a["out"][0:T, :].rearrange("(t p) d -> p t d", p=P)

    with nc.Block() as block:

        @block.sync
        def _(sp):
            for name in ("gate_w", "sh_gate", "sh_up"):
                sp.dma_start(raws[name], a[name].rearrange("(k p) n -> p k n", p=P)).then_inc(w_loaded[name], 16)
            full = GS - 1
            sp.dma_start(down[:, 0:full, :], a["sh_down"][0:full * P, :].rearrange("(g p) n -> p g n", p=P)).then_inc(w_loaded["sh_down"], 16)
            sp.dma_start(down[0:rows[full], full, :], a["sh_down"][full * P:FS, :]).then_inc(w_loaded["sh_down"], 16)
            sp.wait_ge(zero_set, 1)
            sp.dma_start(a["xs"][T:T + P, :], zero[:, :]).then_inc(xn_stored, 16)
            sp.dma_start(a["out"][T:T + P, :], zero[:, 0:D]).then_inc(out_stored, 16)
            for c in range(NCH):
                tiles = slice(TPC * c, TPC * (c + 1))
                sp.wait_ge(ln.xn_ready, TPC * (c + 1))
                sp.dma_start(xn_rows[:, tiles, :], ln.xn[:, :, :]).then_inc(xn_stored, 16)
                sp.wait_ge(scores_ready, c + 1)
                sp.dma_start(score_rows[:, tiles, :], scores[:, :, 0:E]).then_inc(scores_stored, 16)
                for t in range(TPC * c, TPC * (c + 1)):
                    sp.wait_ge(y_added, t + 1)
                    sp.dma_start(out_rows[:, t, :], m.x[:, t, :]).then_inc(out_stored, 16)
            sp.wait_ge(xn_stored, 16 * (NCH + 1))
            sp.wait_ge(scores_stored, 16 * NCH)
            sp.wait_ge(out_stored, 16 * (NT + 1))

        @block.gpsimd
        def _(pool):
            pool.memset(zero[:, :], 0.0).then_inc(zero_set, 1)
            pool.iota(iota_i[:, :], pattern=[[-P, NT]], base=T, channel_multiplier=-1).then_inc(iota_set, 1)
            pool.iota(slot_i[:, :], pattern=[[0, 1]], base=0, channel_multiplier=1).then_inc(iota_set, 1)
            for c in range(NCH):
                ln.gpsimd_rstd(pool, c)

        @block.tensor
        def _(pe):
            def logits_of(c):
                pe.wait_ge(ln.lo_ready, TPC * (c + 1))
                need(pe, y_added, TPC * c - 1)
                product3(pe, m.bank[EB][0:E, :],
                         [(gw_hi[:, k, :], gw_lo[:, k, :], ln.hi[0][:, k, :], ln.lo[0][:, k, :])
                          for k in range(KT)]).then_inc(logits_done, 1)

            def turn_logits(c):
                pe.wait_ge(logits_copied, c + 1)
                need(pe, y_added, TPC * c)
                for j in range(TPC):
                    last = pe.transpose(m.bank[TB][:, j * E:(j + 1) * E], logits_e[:, j * P:(j + 1) * P], m.ident[0:E, 0:E])
                last.then_inc(logits_turned, 1)

            def turn_keys(c):
                pe.wait_ge(keys_ready, TPC * (c + 1))
                for j in range(TPC):
                    last = pe.transpose(m.bank[EB][0:E, j * P:(j + 1) * P], keys[:, j, :], m.ident[:, :])
                last.then_inc(keys_turned, 1)

            for j in range(TPC):
                ln.tensor_turn(pe, 0, j)
            pe.wait_ge(w_ready["gate_w"], 1)
            for c in range(NCH):
                logits_of(c)
                hi, lo = ln.hi[0], ln.lo[0]
                for g in range(GS):
                    n, r = GS * c + g, rows[g]
                    need(pe, hidden_ready, n - 1)
                    for name, bank, done in (("sh_gate", GATEB, gate_done), ("sh_up", UPB, up_done)):
                        if c == 0 and g == 0:
                            pe.wait_ge(w_ready[name], 1)
                        w = slice(g * P, g * P + r)
                        product3(pe, m.bank[bank[n % 2]][0:r, :],
                                 [(w_hi[name][:, k, w], w_lo[name][:, k, w], hi[:, k, :], lo[:, k, :])
                                  for k in range(KT)]).then_inc(done, 1)
                    if g == 0:
                        turn_logits(c)
                    if g == 3:
                        turn_keys(c)
                if c == 0:
                    pe.wait_ge(w_loaded["sh_down"], 32)
                for j in range(TPC):
                    if c + 1 < NCH:
                        ln.tensor_turn(pe, c + 1, j)
                    t = TPC * c + j
                    if j == 0:
                        pe.wait_ge(keys_copied, c + 1)
                        pe.wait_ge(hidden_ready, GS * (c + 1))
                    need(pe, y_added, t - 1)
                    for g in range(GS):
                        r = rows[g]
                        last = pe.matmul(m.bank[DOWNB[t % 2]][:, :], hidden[0:r, g, j * P:(j + 1) * P], down[0:r, g, :],
                                         start=(g == 0), stop=(g == GS - 1))
                    last.then_inc(y_done, 1)
            pe.wait_ge(rank_step, 2 * ROUNDS * NCH)
            pe.wait_ge(y_added, NT - 1)
            pe.transpose(m.bank[EB][:, 0:E], kept[:, :], m.ident[0:E, 0:E]).then_inc(kept_turned, 1)

        @block.scalar
        def _(act):
            def split(name):
                act.wait_ge(w_loaded[name], 16)
                act.activation(parts[name][0][:, :, :], raws[name], ACT.Copy).then_inc(w_hi_ready[name], 1)

            split("gate_w")
            for j in range(TPC):
                ln.scalar_hi(act, 0, j)
            split("sh_gate")
            split("sh_up")
            for c in range(NCH):
                act.wait_ge(logits_done, c + 1)
                need(act, logits_turned, c)
                act.activation(logits_e[:, :], m.bank[EB][0:E, :], ACT.Copy).then_inc(logits_copied, 1)
                for g in range(GS):
                    n, r = GS * c + g, rows[g]
                    if g == 1:
                        act.wait_ge(shifted, c + 1)
                        act.activation(logits[:, :, :], logits[:, :, :], ACT.Exp).then_inc(exp_ready, 1)
                    if g == 4:
                        act.wait_ge(keys_turned, c + 1)
                        need(act, rank_step, 2 * ROUNDS * (c - 1))
                        act.activation(ranks[c % 2][:, CAP:], m.bank[EB][0:E, :], ACT.Copy).then_inc(keys_copied, 1)
                    act.wait_ge(gate_done, n + 1)
                    need(act, hidden_ready, n - 1)
                    act.activation(silu[n % 2][0:r, :], m.bank[GATEB[n % 2]][0:r, :], ACT.Silu).then_inc(silu_ready, 1)
                act.wait_ge(up_done, GS * (c + 1))
                if c + 1 < NCH:
                    for j in range(TPC):
                        ln.scalar_hi(act, c + 1, j)

        @block.vector
        def _(dve):
            def split(name):
                hi, lo = parts[name]
                dve.wait_ge(w_hi_ready[name], 1)
                dve.tensor_tensor(lo[:, :, :], raws[name], hi[:, :, :].bitcast(F32),
                                  ALU.subtract).then_inc(w_ready[name], 1)

            def softmax_shift(c):
                src = m.bank[TB][:, 0:TPC * E].rearrange("p (j e) -> p j e", j=TPC)
                dve.wait_ge(logits_turned, c + 1)
                dve.tensor_reduce(top[:, :], src, AX.X, ALU.max).then_inc(max_ready, 1)
                dve.wait_ge(max_ready, c + 1)
                dve.tensor_tensor(logits[:, :, :], src, top[:, :].unsqueeze(2).to_broadcast([P, TPC, E]),
                                  ALU.subtract).then_inc(shifted, 1)

            def choose(c):
                dve.wait_ge(exp_ready, c + 1)
                dve.tensor_reduce(total[:, :], logits[:, :, :], AX.X, ALU.add).then_inc(sum_ready, 1)
                dve.wait_ge(sum_ready, c + 1)
                dve.reciprocal(total[:, :], total[:, :]).then_inc(inverse_ready, 1)
                dve.wait_ge(inverse_ready, c + 1)
                need(dve, scores_stored, 16 * c)
                dve.tensor_tensor(scores[:, :, 0:E], logits[:, :, :], total[:, :].unsqueeze(2).to_broadcast([P, TPC, E]),
                                  ALU.mult).then_inc(scores_ready, 1)
                dve.wait_ge(scores_ready, c + 1)
                for j in range(TPC):
                    dve.max(best[:, j, :], scores[:, j, 0:E]).then_inc(best_ready, 1)
                dve.wait_ge(best_ready, TPC * (c + 1))
                dve.memset(best[:, :, TOPK:8], SENTINEL).then_inc(best_set, 1)
                dve.wait_ge(best_set, c + 1)
                for j in range(TPC):
                    dve.match_replace(marked[:, j, :], best[:, j, :], scores[:, j, :], -1.0).then_inc(marks_ready, 1)
                need(dve, keys_turned, c)
                for j in range(TPC):
                    t = TPC * c + j
                    dve.wait_ge(marks_ready, t + 1)
                    dve.tensor_scalar(keys[:, j, :], marked[:, j, 0:E], 0.0, key_of[:, t:t + 1],
                                      ALU.is_lt, ALU.mult).then_inc(keys_ready, 1)

            def rank(c, first, last):
                buf = ranks[c % 2]
                for i in range(first, last):
                    n = 2 * (ROUNDS * c + i)
                    if i == 0:
                        dve.wait_ge(keys_copied, c + 1)
                        need(dve, kept_moved, c)
                    need(dve, rank_step, n)
                    dve.max(kept[:, 8 * i:8 * (i + 1)], buf[:, :]).then_inc(rank_step, 1)
                    dve.wait_ge(rank_step, n + 1)
                    dve.match_replace(buf[:, :], kept[:, 8 * i:8 * (i + 1)], buf[:, :], 0.0).then_inc(rank_step, 1)
                if last == ROUNDS and c + 1 < NCH:
                    dve.wait_ge(rank_step, 2 * ROUNDS * (c + 1))
                    dve.tensor_copy(ranks[(c + 1) % 2][:, 0:CAP], kept[:, :]).then_inc(kept_moved, 1)

            def add_y(t):
                dve.wait_ge(y_done, t + 1)
                dve.tensor_tensor(m.x[:, t, :], m.bank[DOWNB[t % 2]][:, :], m.x[:, t, :], ALU.add).then_inc(y_added, 1)

            ln.vector_stats(dve, 0)
            ln.vector_normalize(dve, 0)
            dve.memset(scores[:, :, E:], SENTINEL).then_inc(consts, 1)
            dve.memset(ranks[0][:, 0:CAP], 0.0).then_inc(consts, 1)
            dve.wait_ge(iota_set, 2)
            dve.tensor_copy(key_of[:, :], iota_i[:, :]).then_inc(consts, 1)
            dve.tensor_copy(slot_f[:, :], slot_i[:, :]).then_inc(consts, 1)
            split("gate_w")
            for j in range(TPC):
                ln.vector_lo(dve, 0, j)
            split("sh_gate")
            split("sh_up")
            dve.wait_ge(consts, 4)
            dve.wait_ge(w_ready["sh_gate"], 1)
            for c in range(NCH):
                softmax_shift(c)
                for g in range(GS):
                    n, r = GS * c + g, rows[g]
                    if g == 2:
                        choose(c)
                    if g == 3 and c + 1 < NCH:
                        ln.vector_stats(dve, c + 1)
                    if g == 4 and c + 1 < NCH:
                        dve.wait_ge(xn_stored, 16 * (c + 2))
                        ln.vector_normalize(dve, c + 1)
                    if g == 0:
                        need(dve, y_done, TPC * c)
                    dve.wait_ge(silu_ready, n + 1)
                    dve.wait_ge(up_done, n + 1)
                    dve.tensor_tensor(hidden[0:r, g, :], silu[n % 2][0:r, :], m.bank[UPB[n % 2]][0:r, :],
                                      ALU.mult).then_inc(hidden_ready, 1)
                    if g >= 4:
                        rank(c, 2 * (g - 4), 2 * (g - 3))
                for j in range(TPC):
                    if c + 1 < NCH:
                        ln.vector_lo(dve, c + 1, j)
                    rank(c, 4 + 3 * j, 7 + 3 * j)
                    add_y(TPC * c + j)
            dve.wait_ge(kept_turned, 1)
            turned = m.bank[EB][:, 0:E]
            dve.tensor_scalar(empty[:, :], turned, 0.0, slot_f[:, 0:1], ALU.is_equal, ALU.mult).then_inc(empty_ready, 1)
            dve.tensor_scalar(rows_f[:, :], turned, -1.0, float(T), ALU.mult, ALU.add).then_inc(rows_ready, 1)
            dve.wait_ge(empty_ready, 1)
            dve.wait_ge(rows_ready, 1)
            dve.tensor_tensor(m.slot_rows[:, :], rows_f[:, :], empty[:, :], ALU.add).then_inc(slots_ready, 1)
            dve.wait_ge(slots_ready, 1)


def experts_phase(nc, m, a):
    arena = Arena(nc, m.after_slots)
    R = 4
    GROUPS = E // R
    GF = (F + P - 1) // P
    rows = [min(P, F - g * P) for g in range(GF)]
    w_gate = [arena.put(f"w_gate{i}", [P, KT, F], F32) for i in range(R)]
    w_up = [arena.put(f"w_up{i}", [P, KT, F], F32) for i in range(R)]
    w_down = [arena.put(f"w_down{i}", [P, GF, D], F32) for i in range(R)]
    row_in = [arena.put(f"row_in{i}", [P, 1], U32) for i in range(R)]
    row_out = [arena.put(f"row_out{i}", [P, 1], U32) for i in range(R)]
    AHEAD = 3
    xg = [arena.put(f"xg{i}", [P, XS], F32) for i in range(R)]
    xt = [arena.put(f"xgt{i}", [P, KT, P], F32) for i in range(2)]
    silu = [arena.put(f"e_silu{i}", [P, F], F32) for i in range(2)]
    hidden = [arena.put(f"e_hidden{i}", [P, F], F32) for i in range(2)]
    ht = [arena.put(f"e_ht{i}", [P, GF, P], F32) for i in range(2)]
    y = [arena.put(f"e_y{i}", [P, D], F32) for i in range(2)]
    XB, GATEB, UPB, HB, YB = 0, (1, 2), (3, 4), 5, (6, 7)

    s = nc.alloc_semaphore
    gu_loaded = [s(f"gu_loaded{i}") for i in range(R)]
    down_loaded = [s(f"e_down_loaded{i}") for i in range(R)]
    gathered = [s(f"gathered{i}") for i in range(R)]
    row_in_ready, row_out_ready, x_turned, xt_ready = s("row_in_ready"), s("row_out_ready"), s("e_x_turned"), s("e_xt_ready")
    gate_done, up_done, silu_ready, hidden_ready = s("e_gate_done"), s("e_up_done"), s("e_silu_ready"), s("e_hidden_ready")
    h_turned, ht_ready, down_done, y_ready = s("e_h_turned"), s("e_ht_ready"), s("e_down_done"), s("e_y_ready")
    added = s("expert_added")

    def exists(e):
        return not isinstance(e, int) or 0 <= e < E

    def over_experts(engine, step):
        for e in range(R):
            step(e, e, 0)
        with engine.Fori(1, GROUPS - 1) as g:
            for u in range(R):
                step(g * R + u, u, g)
        for e in range(E - R, E):
            step(e, e % R, GROUPS - 1)

    with nc.Block() as block:

        @block.sync
        def _(sp):
            def step(e, u, g):
                need(sp, up_done, e - R + 1)
                at = lambda w, d: w[bass.ds(e, 1)].rearrange(d, p=P)
                sp.dma_start(w_gate[u][:, :, :], at(a["w_gate"], "o (p k) n -> p (o k) n")).then_inc(gu_loaded[u], 16)
                sp.dma_start(w_up[u][:, :, :], at(a["w_up"], "o (p k) n -> p (o k) n")).then_inc(gu_loaded[u], 16)
                need(sp, down_done, e - R + 1)
                full = GF - 1
                sp.dma_start(w_down[u][:, 0:full, :], a["w_down"][bass.ds(e, 1), 0:full * P, :].rearrange("o (k p) n -> p (o k) n", p=P)).then_inc(down_loaded[u], 16)
                sp.dma_start(w_down[u][0:rows[full], full, :], a["w_down"][bass.ds(e, 1), full * P:F, :].rearrange("o p n -> p (o n)")).then_inc(down_loaded[u], 16)
            over_experts(sp, step)

        @block.gpsimd
        def _(pool):
            def gather(e, u):
                need(pool, y_ready, e - R + 1)
                wait_apart(pool, row_in_ready, e + 1, row_in_ready)
                pool.indirect_dma_start(out=xg[u][:, :], out_offset=None, in_=a["xs"][:, :],
                                        in_offset=bass.IndirectOffsetOnAxis(ap=row_in[u][:, :], axis=0)).then_inc(gathered[u], 16)

            def step(e, u, g):
                if exists(e + AHEAD):
                    gather(e + AHEAD, (u + AHEAD) % R)
                pool.wait_ge(row_out_ready, e + 1)
                pool.wait_ge(y_ready, e + 1)
                wait_apart(pool, added, 16 * e, row_out_ready)
                pool.indirect_dma_start(out=a["out"][:, :], out_offset=bass.IndirectOffsetOnAxis(ap=row_out[u][:, :], axis=0),
                                        in_=y[u % 2][:, :], in_offset=None, compute_op=ALU.add).then_inc(added, 16)
            for e in range(AHEAD):
                gather(e, e)
            over_experts(pool, step)
            pool.wait_ge(added, 16 * E)

        @block.tensor
        def _(pe):
            def turn_x(e, u, g):
                pe.wait_ge(gathered[u], 16 * (g + 1))
                need(pe, xt_ready, e)
                for k in range(KT):
                    last = pe.transpose(m.bank[XB][:, k * P:(k + 1) * P], xg[u][:, k:D:KT], m.ident[:, :])
                last.then_inc(x_turned, 1)

            def down(e, u, g):
                pe.wait_ge(ht_ready, e + 1)
                pe.wait_ge(down_loaded[u], 32 * (g + 1))
                need(pe, y_ready, e - 1)
                for k in range(GF):
                    r = rows[k]
                    last = pe.matmul(m.bank[YB[u % 2]][:, :], ht[u % 2][0:r, k, :], w_down[u][0:r, k, :],
                                     start=(k == 0), stop=(k == GF - 1))
                last.then_inc(down_done, 1)

            def step(e, u, g):
                if exists(e + 1):
                    turn_x(e + 1, (u + 1) % R, g if u < R - 1 else g + 1)
                pe.wait_ge(xt_ready, e + 1)
                pe.wait_ge(gu_loaded[u], 32 * (g + 1))
                need(pe, hidden_ready, e - 1)
                for w, bank, done in ((w_gate, GATEB, gate_done), (w_up, UPB, up_done)):
                    for k in range(KT):
                        last = pe.matmul(m.bank[bank[u % 2]][:, 0:F], xt[u % 2][:, k, :], w[u][:, k, :],
                                         start=(k == 0), stop=(k == KT - 1))
                    last.then_inc(done, 1)
                if exists(e - 1):
                    down(e - 1, (u - 1) % R, g if u else g - 1)
                pe.wait_ge(hidden_ready, e + 1)
                need(pe, ht_ready, e)
                for k in range(GF):
                    r = rows[k]
                    last = pe.transpose(m.bank[HB][0:r, k * P:(k + 1) * P], hidden[u % 2][:, k * P:k * P + r], m.ident[:, :])
                last.then_inc(h_turned, 1)

            turn_x(0, 0, 0)
            over_experts(pe, step)
            down(E - 1, R - 1, GROUPS - 1)

        @block.scalar
        def _(act):
            def weigh(e, u):
                act.wait_ge(down_done, e + 1)
                need(act, added, 16 * (e - 1))
                act.activation(y[u % 2][:, :], m.bank[YB[u % 2]][:, :], ACT.Copy,
                               scale=xg[u][:, bass.ds(D + e, 1)]).then_inc(y_ready, 1)

            def step(e, u, g):
                act.wait_ge(gate_done, e + 1)
                need(act, hidden_ready, e - 1)
                act.activation(silu[u % 2][:, :], m.bank[GATEB[u % 2]][:, 0:F], ACT.Silu).then_inc(silu_ready, 1)
                if exists(e - 1):
                    weigh(e - 1, (u - 1) % R)
            over_experts(act, step)
            weigh(E - 1, R - 1)

        @block.vector
        def _(dve):
            def copy_row_in(e, u, g):
                if not isinstance(e, int) or e >= R:
                    wait_apart(dve, gathered[u], 16 * g, row_in_ready)
                dve.tensor_copy(row_in[u][:, :], m.slot_rows[:, bass.ds(e, 1)]).then_inc(row_in_ready, 1)

            def copy_row_out(e, u):
                wait_apart(dve, added, 16 * (e - R + 1), row_in_ready)
                dve.tensor_copy(row_out[u][:, :], m.slot_rows[:, bass.ds(e, 1)]).then_inc(row_out_ready, 1)

            def copy_x(e, u):
                dve.wait_ge(x_turned, e + 1)
                need(dve, up_done, e - 1)
                dve.tensor_copy(xt[u % 2][:, :, :], m.bank[XB][:, :].rearrange("p (k n) -> p k n", k=KT)).then_inc(xt_ready, 1)

            def step(e, u, g):
                if exists(e + 1):
                    copy_x(e + 1, (u + 1) % R)
                if exists(e + AHEAD):
                    copy_row_in(e + AHEAD, (u + AHEAD) % R, g + (u + AHEAD) // R)
                copy_row_out(e, u)
                dve.wait_ge(silu_ready, e + 1)
                dve.wait_ge(up_done, e + 1)
                need(dve, h_turned, e - 1)
                dve.tensor_tensor(hidden[u % 2][:, :], silu[u % 2][:, :], m.bank[UPB[u % 2]][:, 0:F],
                                  ALU.mult).then_inc(hidden_ready, 1)
                dve.wait_ge(h_turned, e + 1)
                need(dve, down_done, e - 1)
                for k in range(GF):
                    r = rows[k]
                    last = dve.tensor_copy(ht[u % 2][0:r, k, :], m.bank[HB][0:r, k * P:(k + 1) * P])
                last.then_inc(ht_ready, 1)

            for e in range(AHEAD):
                copy_row_in(e, e, 0)
            copy_x(0, 0)
            over_experts(dve, step)


PHASES = [qkv_phase, attention_phase, ffn_phase, recurrence_phase, router_phase, experts_phase]


def build(nc, a):
    m = setup_memory(nc, a)
    for phase in PHASES:
        free = list(nc.free_semaphores)
        phase(nc, m, a)
        left = set(nc.free_semaphores)
        nc.clear_and_free_semaphores([i for i in free if i not in left])
        nc.all_engine_barrier()


def kernel(**inputs):
    import numpy as np
    import concourse.bacc as bacc
    from concourse.bass_utils import run_bass_kernel_spmd

    def np_of(name):
        return np.asarray(inputs[name])

    def nibble_order(w, axis):
        w = np.moveaxis(w, axis, 0)
        w = w.reshape(w.shape[0] // P, 16, 8, *w.shape[1:]).swapaxes(1, 2).reshape(w.shape)
        return np.moveaxis(w, 0, axis)

    def columns(words):
        return words.reshape(-1, 16, words.shape[1]).swapaxes(0, 1).reshape(16, -1)

    gu, gus = np_of("L0_ffn_gate_up_packed"), np_of("L0_ffn_gate_up_scales")
    arrays = {
        "x": np_of("L0_attn_x").reshape(T, D),
        "wqkv": np_of("L0_attn_Wqkv"),
        "bqkv": np_of("L0_attn_bqkv"),
        "wo": np_of("L0_attn_Wo"),
        "bo": np_of("L0_attn_bo"),
        "fp4_words": np.tile(np.concatenate([columns(nibble_order(gu, 0).T),
                                             columns(np_of("L0_ffn_down_packed").T)], 1), (8, 1)),
        "fp4_scales": np.concatenate([nibble_order(gus, 1).ravel(), np_of("L0_ffn_down_scales").ravel()]),
        "w_in": np_of("L1_attn_W_in").T,
        "w_out": np_of("L1_attn_W_out").T,
        "decay": np_of("L1_attn_decay"),
        "b1": np_of("L1_attn_bias"),
        "gate_w": np_of("L1_ffn_gate_w").T,
        "w_gate": np_of("L1_ffn_w_gate"),
        "w_up": np_of("L1_ffn_w_up"),
        "w_down": np_of("L1_ffn_w_down"),
        "sh_gate": np_of("L1_ffn_sh_gate").T,
        "sh_up": np_of("L1_ffn_sh_up").T,
        "sh_down": np_of("L1_ffn_sh_down").T,
    }
    nc = bacc.Bacc("TRN2", target_bir_lowering=False, num_devices=1)
    a, maps = {}, {}
    for name, v in arrays.items():
        v = np.ascontiguousarray(v)
        maps[f"in_{name}"] = v
        a[name] = nc.dram_tensor(f"in_{name}", v.shape, mybir.dt.from_np(v.dtype), kind="ExternalInput").ap()
    a["out"] = nc.dram_tensor("out_x", (T + P, D), F32, kind="ExternalOutput").ap()
    a["qk"] = nc.dram_tensor("qk_parts", (2, B, 2, D, S), F32).ap()
    a["fp4_out"] = nc.dram_tensor("fp4_out", (3, P, GU_COLS + DOWN_COLS), F32).ap()
    a["xs"] = nc.dram_tensor("expert_rows", (T + P, XS), F32).ap()
    build(nc, a)
    r = run_bass_kernel_spmd(nc, [maps], core_ids=[0])
    return r.results[0]["out_x"][:T].reshape(B, S, D)
```

```python
import concourse.bass as bass
from concourse import mybir

ALU = mybir.AluOpType
ACT = mybir.ActivationFunctionType
AX = mybir.AxisListType
F32 = mybir.dt.float32
F32R = mybir.dt.float32r
BF16 = mybir.dt.bfloat16
F16 = mybir.dt.float16
I32 = mybir.dt.int32
U32 = mybir.dt.uint32

P = 128
B, S, D = 2, 1024, 512
T = B * S
NT = T // P
CH = 512
NCH = T // CH
TPC = CH // P
KT = D // P
H, HD = 16, 32
I0 = 1408
G0 = I0 // P
E, F, CAP, TOPK = 64, 352, 128, 6
FS = 2 * F
LN_EPS = 1e-5
RMS_EPS = 1e-6
XS = D + E
NEG = -1e30


SBUF_END = 229344


class Memory:
    pass


class Arena:

    def __init__(self, nc, at=0):
        self.nc, self.at = nc, at

    def put(self, name, shape, dtype):
        size = mybir.dt.size(dtype)
        for n in shape[1:]:
            size *= n
        t = self.nc.alloc_sbuf_tensor_at(name, shape, dtype, offset=self.at)
        self.at += (size + 31) // 32 * 32
        return t


def setup_memory(nc, a):
    m = Memory()
    start = (nc.sbuf_base + 31) // 32 * 32
    arena = Arena(nc, start)
    m.x = arena.put("x_residual", [P, NT, D], F32)
    m.ident = arena.put("ident", [P, P], F32)
    m.ident16 = arena.put("ident16", [P, P], BF16)
    m.mask_qk = arena.put("mask_qk", [P, P], BF16)
    m.mask_kq = arena.put("mask_kq", [P, P], BF16)
    m.bqk = arena.put("bqk", [P, 2 * KT], F32)
    m.attention_rows = arena.at
    m.bv = arena.put("bv_rows", [P, D], F32)
    m.bo = arena.put("bo_rows", [P, D], F32)
    m.b1 = arena.put("b1_rows", [P, D], F32)
    m.stats = arena.put("ln_stats", [P, TPC, 6], F32)
    m.mv = arena.put("ln_mean_var", [P, TPC, 2], F32)
    m.rstd = arena.put("ln_rstd", [P, TPC], F32)
    m.base = arena.at
    top = Arena(nc, SBUF_END - 4 * (TPC * D + 2 * KT * CH))
    m.ln_xn = top.put("ln_xn", [P, TPC, D], F32)
    m.ln_hi = top.put("ln_xt_hi", [P, KT, CH], F32R)
    m.ln_lo = top.put("ln_xt_lo", [P, KT, CH], F32R)
    m.bank = [nc.alloc_psum_tensor(f"bank{i}", [P, 512], F32) for i in range(8)]
    return m


class InverseRoot:

    STEPS = 3

    def __init__(self, nc, arena, tag, n):
        self.v = arena.put(f"{tag}_root_v", [P, n], F32)
        self.half = arena.put(f"{tag}_root_half", [P, n], I32)
        self.y0 = arena.put(f"{tag}_root_y0", [P, n], I32)
        self.y = arena.put(f"{tag}_root_y", [P, n], F32)
        self.t = arena.put(f"{tag}_root_t", [P, n], F32)
        self.v_ready = nc.alloc_semaphore(f"{tag}_root_v_ready")
        self.half_ready = nc.alloc_semaphore(f"{tag}_root_half_ready")
        self.ready = nc.alloc_semaphore(f"{tag}_root_guess_ready")
        self.step = nc.alloc_semaphore(f"{tag}_root_step")
        self.guesses = self.steps = 0

    def vector_guess(self, dve, src, scale, eps):
        self.guesses += 1
        dve.tensor_scalar(self.v[:, :], src, scale, eps, ALU.mult, ALU.add).then_inc(self.v_ready, 1)
        dve.wait_ge(self.v_ready, self.guesses)
        dve.tensor_scalar(self.half[:, :], self.v[:, :].bitcast(I32), 1, 0, ALU.logical_shift_right,
                          ALU.bitwise_or).then_inc(self.half_ready, 1)
        dve.wait_ge(self.half_ready, self.guesses)
        dve.tensor_scalar(self.y0[:, :], self.half[:, :], -1.0, float(0x5F3759DF), ALU.mult,
                          ALU.add).then_inc(self.ready, 1)

    def gpsimd_refine(self, pool, out, out_ready):
        def then(instruction):
            self.steps += 1
            instruction.then_inc(self.step, 1)
            pool.wait_ge(self.step, self.steps)

        y = self.y0[:, :].bitcast(F32)
        for n in range(self.STEPS):
            then(pool.tensor_tensor(self.t[:, :], y, y, ALU.mult))
            then(pool.tensor_tensor(self.t[:, :], self.t[:, :], self.v[:, :], ALU.mult))
            then(pool.tensor_scalar(self.t[:, :], self.t[:, :], -0.5, 1.5, ALU.mult, ALU.add))
            if n < self.STEPS - 1:
                then(pool.tensor_tensor(self.y[:, :], y, self.t[:, :], ALU.mult))
                y = self.y[:, :]
            else:
                pool.tensor_tensor(out, y, self.t[:, :], ALU.mult).then_inc(out_ready, 1)


class LayerNorm:

    def __init__(self, nc, m, arena, tag, banks=(0, 1), buffers=2, first=0, nibbles=()):
        self.nc, self.m, self.banks, self.buffers, self.nibbles, self.first = nc, m, banks, buffers, nibbles, first
        self.xn = m.ln_xn
        self.hi = [m.ln_hi] + [arena.put(f"{tag}_xt_hi{i}", [P, KT, CH], F32R) for i in range(1, buffers)]
        self.lo = [m.ln_lo] + [arena.put(f"{tag}_xt_lo{i}", [P, KT, CH], F32R) for i in range(1, buffers)]
        s = lambda name: nc.alloc_semaphore(f"{tag}_{name}")
        self.guess = InverseRoot(nc, arena, tag, TPC)
        self.stats_ready, self.mean_ready = s("stats_ready"), s("mean_ready")
        self.rstd_ready, self.xn_ready = s("rstd_ready"), s("xn_ready")
        self.turned, self.hi_ready, self.lo_ready = s("turned"), s("hi_ready"), s("lo_ready")

    def wait_xn(self, engine, c):
        need(engine, self.xn_ready, TPC * (c + 1 - self.first))

    def wait_lo(self, engine, c):
        need(engine, self.lo_ready, TPC * (c + 1 - self.first))

    def vector_stats(self, dve, c):
        m, n = self.m, c - self.first
        need(dve, self.xn_ready, TPC * n)
        for j in range(TPC):
            dve.bn_stats(m.stats[:, j, :], m.x[:, (TPC * c + j) % NT, :]).then_inc(self.stats_ready, 1)
        for j in range(TPC):
            dve.wait_ge(self.stats_ready, TPC * n + j + 1)
            dve.bn_aggr(m.mv[:, j, :], m.stats[:, j, :]).then_inc(self.mean_ready, 1)
        dve.wait_ge(self.mean_ready, TPC * (n + 1))
        need(dve, self.rstd_ready, n)
        self.guess.vector_guess(dve, m.mv[:, :, 1], 1.0, LN_EPS)

    def gpsimd_rstd(self, pool, c):
        pool.wait_ge(self.guess.ready, c + 1 - self.first)
        self.guess.gpsimd_refine(pool, self.m.rstd[:, :], self.rstd_ready)

    def vector_normalize(self, dve, c):
        for j in range(TPC):
            self.vector_normalize_tile(dve, c, j)

    def vector_normalize_tile(self, dve, c, j):
        m, n = self.m, c - self.first
        if j == 0:
            dve.wait_ge(self.rstd_ready, n + 1)
        if n >= 1:
            dve.wait_ge(self.turned, TPC * (n - 1) + j + 1)
        out, x = self.xn[:, j, :], m.x[:, (TPC * c + j) % NT, :]
        if c in self.nibbles:
            out = out.rearrange("p (k i w) -> p k i w", i=8, w=16)
            x = x.rearrange("p (k w i) -> p k i w", i=8, w=16)
        dve.tensor_scalar(out, x, m.mv[:, j, 0:1], m.rstd[:, j:j + 1],
                          ALU.subtract, ALU.mult).then_inc(self.xn_ready, 1)

    def tensor_turn(self, pe, c, j):
        t = TPC * (c - self.first) + j
        bank = self.m.bank[self.banks[t % 2]]
        pe.wait_ge(self.xn_ready, t + 1)
        need(pe, self.lo_ready, t - 1)
        for k in range(KT):
            last = pe.transpose(bank[:, k * P:(k + 1) * P], self.xn[:, j, k * P:(k + 1) * P], self.m.ident[:, :])
        last.then_inc(self.turned, 1)

    def scalar_hi(self, act, c, j):
        t = TPC * (c - self.first) + j
        act.wait_ge(self.turned, t + 1)
        src = self.m.bank[self.banks[t % 2]][:, :].rearrange("p (k n) -> p k n", k=KT)
        act.activation(self.hi[c % self.buffers][:, :, j * P:(j + 1) * P], src, ACT.Copy).then_inc(self.hi_ready, 1)

    def vector_lo(self, dve, c, j):
        t = TPC * (c - self.first) + j
        dve.wait_ge(self.hi_ready, t + 1)
        src = self.m.bank[self.banks[t % 2]][:, :].rearrange("p (k n) -> p k n", k=KT)
        b, cols = c % self.buffers, slice(j * P, (j + 1) * P)
        dve.tensor_tensor(self.lo[b][:, :, cols], src, self.hi[b][:, :, cols].bitcast(F32),
                          ALU.subtract).then_inc(self.lo_ready, 1)


def product3(pe, out, terms, start=True, stop=True):
    n = len(terms)
    for i, (sh, sl, mh, ml) in enumerate(terms):
        pe.matmul(out, sh, mh, start=start and i == 0, stop=False)
        pe.matmul(out, sh, ml, start=False, stop=False)
        last = pe.matmul(out, sl, mh, start=False, stop=stop and i == n - 1)
    return last


def qkv_phase(nc, m, a):
    arena = Arena(nc, m.base)
    m.v = arena.put("v_all", [P, B * H, S // P, HD], F32)
    m.after_v = arena.at
    w_raw = arena.put("wqkv_raw", [P, KT, 3 * D], F32)
    w_hi = arena.put("wqkv_hi", [P, KT, 3 * D], F32R)
    w_lo = arena.put("wqkv_lo", [P, KT, 3 * D], F32R)
    ln = LayerNorm(nc, m, arena, "ln1")
    STAGES = 4
    st_hi = [arena.put(f"qk_stage_hi{i}", [P, CH], F32R) for i in range(STAGES)]
    st_lo = [arena.put(f"qk_stage_lo{i}", [P, CH], F32R) for i in range(STAGES)]

    s = nc.alloc_semaphore
    x_loaded = [s(f"x_loaded{c}") for c in range(NCH)]
    w_loaded = [s(f"wqkv_loaded{k}") for k in range(KT)]
    w_hi_ready, w_lo_ready = s("wqkv_hi_ready"), s("wqkv_lo_ready")
    ident_set, consts_ready = s("ident_set"), s("consts_ready")
    bias_loaded = s("bias_loaded")
    product_done, hi_ready, unit_used = s("qkv_product_done"), s("qk_hi_ready"), s("qkv_unit_used")
    stored = [s(f"qk_stored{i}") for i in range(STAGES)]
    UNITS = 2 * KT + TPC
    FIRST, BANKS = 2, 6

    with nc.Block() as block:

        @block.sync
        def _(sp):
            xv = a["x"].rearrange("(t p) d -> p t d", p=P)
            for c in range(NCH):
                sp.dma_start(m.x[:, TPC * c:TPC * (c + 1), :], xv[:, TPC * c:TPC * (c + 1), :]).then_inc(x_loaded[c], 16)
                if c == 0:
                    for k in range(KT):
                        sp.dma_start(w_raw[:, k, :], a["wqkv"][k * P:(k + 1) * P, :]).then_inc(w_loaded[k], 16)
                    with nc.allow_non_contiguous_dma("eight small bias columns"):
                        sp.dma_start(m.bqk[:, :], a["bqkv"][0:2 * D].rearrange("(n p) -> p n", p=P)).then_inc(bias_loaded, 16)
                    sp.dma_start(m.bv[:, :], a["bqkv"][2 * D:3 * D].partition_broadcast(P)).then_inc(bias_loaded, 16)
                    sp.dma_start(m.bo[:, :], a["bo"].partition_broadcast(P)).then_inc(bias_loaded, 16)
                    sp.dma_start(m.b1[:, :], a["b1"].partition_broadcast(P)).then_inc(bias_loaded, 16)
            q = 0
            for c in range(NCH):
                b, col = c // 2, (c % 2) * CH
                for n in range(2 * KT):
                    sp.wait_ge(unit_used, UNITS * c + n + 1)
                    which, o = n // KT, n % KT
                    for half, st in ((0, st_hi), (1, st_lo)):
                        sp.dma_start(a["qk"][which, half, b, o * P:(o + 1) * P, col:col + CH],
                                     st[q % STAGES][:, :].bitcast(F32)).then_inc(stored[q % STAGES], 16)
                    q += 1
            for i in range(STAGES):
                sp.wait_ge(stored[i], 32 * (q // STAGES))

        @block.gpsimd
        def _(pool):
            pool.memset(m.ident[:, :], 0.0).then_inc(ident_set, 1)
            pool.memset(m.ident16[:, :], 0.0).then_inc(ident_set, 1)
            pool.memset(m.mask_qk[:, :], 0.0).then_inc(ident_set, 1)
            pool.memset(m.mask_kq[:, :], 0.0).then_inc(ident_set, 1)
            pool.wait_ge(ident_set, 4)
            for t in (m.ident, m.ident16):
                pool.affine_select(out=t[:, :], in_=t[:, :], compare_op=ALU.not_equal, fill=1.0, base=0,
                                   pattern=[[-1, P]], channel_multiplier=1).then_inc(consts_ready, 1)
            pool.affine_select(out=m.mask_qk[:, :], in_=m.mask_qk[:, :], compare_op=ALU.is_ge, fill=NEG, base=0,
                               pattern=[[-1, P]], channel_multiplier=1).then_inc(consts_ready, 1)
            pool.affine_select(out=m.mask_kq[:, :], in_=m.mask_kq[:, :], compare_op=ALU.is_ge, fill=NEG, base=0,
                               pattern=[[1, P]], channel_multiplier=-1).then_inc(consts_ready, 1)
            for c in range(NCH):
                ln.gpsimd_rstd(pool, c)

        @block.tensor
        def _(pe):
            pe.wait_ge(consts_ready, 4)
            for j in range(TPC):
                ln.tensor_turn(pe, 0, j)
            for c in range(NCH):
                hi, lo = ln.hi[c % 2], ln.lo[c % 2]
                pe.wait_ge(ln.lo_ready, TPC * (c + 1))
                if c == 0:
                    pe.wait_ge(w_lo_ready, KT)
                for n in range(UNITS):
                    u = UNITS * c + n
                    if u >= BANKS:
                        pe.wait_ge(unit_used, u - BANKS + 1)
                    bank = m.bank[FIRST + u % BANKS]
                    if n < 2 * KT:
                        w = slice(n * P, (n + 1) * P)
                        terms = [(w_hi[:, k, w], w_lo[:, k, w], hi[:, k, :], lo[:, k, :]) for k in range(KT)]
                    else:
                        tok = slice((n - 2 * KT) * P, (n - 2 * KT + 1) * P)
                        terms = [(hi[:, k, tok], lo[:, k, tok], w_hi[:, k, 2 * D:], w_lo[:, k, 2 * D:]) for k in range(KT)]
                    product3(pe, bank[:, :], terms).then_inc(product_done, 1)
                    if c + 1 < NCH and n in (5, 6, 7, 8):
                        ln.tensor_turn(pe, c + 1, n - 5)

        @block.scalar
        def _(act):
            for k in range(KT):
                act.wait_ge(w_loaded[k], 16)
                act.activation(w_hi[:, k, :], w_raw[:, k, :], ACT.Copy).then_inc(w_hi_ready, 1)
            for j in range(TPC):
                ln.scalar_hi(act, 0, j)
            act.wait_ge(bias_loaded, 64)
            q = 0
            for c in range(NCH):
                for n in range(UNITS):
                    u = UNITS * c + n
                    if n < 2 * KT:
                        act.wait_ge(product_done, u + 1)
                        if q >= STAGES:
                            act.wait_ge(stored[q % STAGES], 32 * (q // STAGES))
                        act.activation(st_hi[q % STAGES][:, :], m.bank[FIRST + u % BANKS][:, :], ACT.Identity,
                                       bias=m.bqk[:, n:n + 1]).then_inc(hi_ready, 1)
                        q += 1
                    if c + 1 < NCH and n in (5, 6, 7, 8):
                        ln.scalar_hi(act, c + 1, n - 5)

        @block.vector
        def _(dve):
            dve.wait_ge(x_loaded[0], 16)
            ln.vector_stats(dve, 0)
            ln.vector_normalize(dve, 0)
            for j in range(TPC):
                ln.vector_lo(dve, 0, j)
            for k in range(KT):
                dve.wait_ge(w_hi_ready, k + 1)
                dve.tensor_tensor(w_lo[:, k, :], w_raw[:, k, :], w_hi[:, k, :].bitcast(F32),
                                  ALU.subtract).then_inc(w_lo_ready, 1)
            dve.wait_ge(bias_loaded, 64)
            q = 0
            for c in range(NCH):
                if c + 1 < NCH:
                    dve.wait_ge(x_loaded[c + 1], 16)
                    ln.vector_stats(dve, c + 1)
                for n in range(UNITS):
                    u = UNITS * c + n
                    bank = m.bank[FIRST + u % BANKS]
                    if n < 2 * KT:
                        dve.wait_ge(hi_ready, q + 1)
                        dve.scalar_tensor_tensor(out=st_lo[q % STAGES][:, :], in0=bank[:, :], scalar=m.bqk[:, n:n + 1],
                                                 in1=st_hi[q % STAGES][:, :].bitcast(F32), op0=ALU.add,
                                                 op1=ALU.subtract).then_inc(unit_used, 1)
                        q += 1
                    else:
                        dve.wait_ge(product_done, u + 1)
                        b, kt = c // 2, TPC * (c % 2) + n - 2 * KT
                        rows = lambda x: x.rearrange("p (h d) -> p h d", h=H)
                        dve.tensor_tensor(m.v[:, H * b:H * (b + 1), kt, :], rows(bank[:, :]), rows(m.bv[:, :]),
                                          ALU.add).then_inc(unit_used, 1)
                    if c + 1 < NCH:
                        if n == 2:
                            ln.vector_normalize(dve, c + 1)
                        if n in (5, 6, 7, 8):
                            ln.vector_lo(dve, c + 1, n - 5)


def need(engine, semaphore, value):
    if not isinstance(value, int) or value > 0:
        engine.wait_ge(semaphore, value)


def wait_apart(engine, semaphore, value, passed):
    if not isinstance(value, int):
        value = engine.to_reg(value)
    engine.wait_ge(passed, 1)
    need(engine, semaphore, value)


SLICES = 32
GU_COLS, DOWN_COLS = KT * 2 * I0, G0 * D
SLICE = (GU_COLS + DOWN_COLS) // SLICES


class Dequantizer:

    def __init__(self, nc, m, a, arena):
        self.a = a
        put = arena.put
        self.words = [put(f"fp4_words{i}", [P, SLICE], I32) for i in range(2)]
        self.scales = [put(f"fp4_scales{i}", [P, SLICE], F16) for i in range(2)]
        self.bits, self.sign = put("fp4_bits", [P, SLICE], I32), put("fp4_sign", [P, SLICE], I32)
        self.codes, self.bent = put("fp4_codes", [P, SLICE], F32), put("fp4_bent", [P, SLICE], F32)
        self.w = put("fp4_w", [P, SLICE], F32)
        self.hi, self.lo = put("fp4_hi", [P, SLICE], F32R), put("fp4_lo", [P, SLICE], F32)
        self.shift, self.shift3 = put("fp4_shift", [P, 1], I32), put("fp4_shift3", [P, 1], I32)
        s = nc.alloc_semaphore
        self.loaded = [s("fp4_loaded0"), s("fp4_loaded1")]
        self.index_ready, self.shift_ready = s("fp4_index_ready"), s("fp4_shift_ready")
        self.nibbles_ready, self.nibbles_used = s("fp4_nibbles_ready"), s("fp4_nibbles_used")
        self.hi_ready = s("fp4_hi_ready")
        self.step, self.w_ready, self.stored = s("fp4_step"), s("fp4_w_ready"), s("fp4_stored")

    def gpsimd_shifts(self, pool):
        pool.iota(self.shift[:, :], [[0, 1]], base=0, channel_multiplier=1).then_inc(self.index_ready, 1)

    def vector_shifts(self, dve):
        dve.wait_ge(self.index_ready, 1)
        dve.tensor_scalar(self.shift[:, :], self.shift[:, :], 4, 2, ALU.logical_shift_right,
                          ALU.logical_shift_left).then_inc(self.shift_ready, 1)
        dve.wait_ge(self.shift_ready, 1)
        dve.tensor_scalar(self.shift3[:, :], self.shift[:, :], 3.0, None, ALU.add).then_inc(self.shift_ready, 1)

    def sync_load(self, sp, h, u):
        need(sp, self.nibbles_used, h - 1)
        cols, b = bass.ds(h * SLICE, SLICE), u % 2
        sp.dma_start(self.words[b][:, :], self.a["fp4_words"][:, cols]).then_inc(self.loaded[b], 16)
        sp.dma_start(self.scales[b][:, :], self.a["fp4_scales"][cols].partition_broadcast(P)).then_inc(self.loaded[b], 16)

    def vector_nibbles(self, dve, g, u, h):
        if isinstance(h, int) and h == 0:
            dve.wait_ge(self.shift_ready, 2)
        b = u % 2
        dve.wait_ge(self.loaded[b], 32 * (2 * g + u // 2 + 1))
        need(dve, self.nibbles_used, h)
        dve.tensor_scalar(self.bits[:, :], self.words[b][:, :], self.shift[:, :], 7, ALU.logical_shift_right,
                          ALU.bitwise_and).then_inc(self.nibbles_ready, 1)

    def vector_signs(self, dve, u):
        b = u % 2
        dve.tensor_scalar(self.sign[:, :], self.words[b][:, :], self.shift3[:, :], 1, ALU.logical_shift_right,
                          ALU.bitwise_and).then_inc(self.nibbles_ready, 1)

    def vector_codes(self, dve, h):
        dve.wait_ge(self.nibbles_ready, 3 * h + 1)
        dve.scalar_tensor_tensor(out=self.codes[:, :], in0=self.bits[:, :], scalar=4.0, in1=self.bits[:, :],
                                 op0=ALU.max, op1=ALU.add).then_inc(self.nibbles_ready, 1)

    def gpsimd_values(self, pool, h, u):
        STEPS = 4
        done = 0

        def then(instruction):
            nonlocal done
            done += 1
            instruction.then_inc(self.step, 1)
            wait_apart(pool, self.step, h * STEPS + done, self.index_ready)

        wait_apart(pool, self.nibbles_ready, 3 * (h + 1), self.index_ready)
        then(pool.tensor_scalar(self.bent[:, :], self.codes[:, :], 12.0, -16.0, ALU.max, ALU.add))
        then(pool.tensor_tensor(self.codes[:, :], self.codes[:, :], self.bent[:, :], ALU.add))
        then(pool.tensor_scalar(self.bent[:, :], self.sign[:, :], -1.0, 0.5, ALU.mult, ALU.add))
        then(pool.tensor_tensor(self.bent[:, :], self.bent[:, :], self.scales[u % 2][:, :], ALU.mult))
        need(pool, self.stored, 48 * h)
        pool.tensor_tensor(self.w[:, :], self.codes[:, :], self.bent[:, :], ALU.mult).then_inc(self.nibbles_used, 1)

    def scalar_hi(self, act, h):
        act.wait_ge(self.nibbles_used, h + 1)
        need(act, self.stored, 48 * h)
        act.activation(self.hi[:, :], self.w[:, :], ACT.Copy).then_inc(self.hi_ready, 1)

    def vector_lo(self, dve, h):
        dve.wait_ge(self.hi_ready, h + 1)
        dve.tensor_tensor(self.lo[:, :], self.w[:, :], self.hi[:, :].bitcast(F32), ALU.subtract).then_inc(self.w_ready, 1)

    def sync_store(self, sp, h):
        sp.wait_ge(self.w_ready, h + 1)
        cols = bass.ds(h * SLICE, SLICE)
        for n, t in enumerate((self.w, self.hi, self.lo)):
            sp.dma_start(self.a["fp4_out"][n, :, cols], t[:, :].bitcast(F32)).then_inc(self.stored, 16)


def attention_phase(nc, m, a):
    QT = S // P
    HEADS = B * H
    SLOTS = 4
    AHEAD = 2
    ROWS = 3 * HD
    scale = HD ** -0.5
    MAX_UNITS = [(q, half, min(CH, (q + 1) * P - half * CH)) for q in range(QT) for half in range(1 + q // TPC)]
    EXP_UNITS = [(k, max(k * P, c * CH), (c + 1) * CH - max(k * P, c * CH)) for c in range(2) for k in range((c + 1) * TPC)]
    N = len(MAX_UNITS)
    assert N == len(EXP_UNITS) and N % 6 == 0
    LAG = 2
    LAST0 = max(i for i, (k, q0, n) in enumerate(EXP_UNITS) if q0 < CH)
    MAXB, EXPB, OUTB = (0, 1, 7), (2, 3, 4), (5, 6)
    TURNED = (OUTB[0], slice(2 * HD, 2 * HD + 2 * QT))
    EXPS = 6
    LN_TURN = 9
    PIECES = 8
    NIBBLES_AT = 3
    PIECE_AT = {(SLOTS - 1, 9): 0, (SLOTS - 1, 11): 1, (0, 1): 2, (0, 4): 3, (0, 6): 4, (0, 8): 5, (0, 11): 6, (1, 1): 7}

    arena = Arena(nc, m.after_v)
    m.attn = arena.put("attn_t", [P, HEADS // SLOTS, S], F32)
    wo_raw = Arena(nc, arena.at - 4 * KT * D).put("wo_raw", [P, KT, D], F32)
    wo_hi = arena.put("wo_hi", [P, KT, D], F32R)
    wo_lo = arena.put("wo_lo", [P, KT, D], F32R)
    probs = [arena.put(f"probs{i}", [P, CH], F32) for i in range(EXPS)]
    parts = [arena.put(f"max_parts{i}", [P, 2, QT], F32) for i in range(2)]
    top = arena.put("neg_max", [P, 2, QT], F32)
    top_t = [arena.put(f"neg_max_t{i}", [2 * QT, P], F32R) for i in range(2)]
    vs = [arena.put(f"v_ones{i}", [P, QT, 2 * HD], F32) for i in range(SLOTS)]
    out_t = arena.put("out_t", [P, S], F32)
    sums_t = arena.put("sums_t", [P, S], F32)
    dq = Dequantizer(nc, m, a, arena)
    ln = LayerNorm(nc, m, arena, "ln2_first", buffers=1, first=NCH, nibbles=(NCH,))
    stacks_at = SBUF_END - 2 * SLOTS * 4 * S
    assert arena.at <= stacks_at
    arena = Arena(nc, stacks_at)
    qs = [arena.put(f"q_stack{i}", [P, S], F32R) for i in range(SLOTS)]
    ks = [arena.put(f"k_stack{i}", [P, S], F32R) for i in range(SLOTS)]
    arena = Arena(nc, stacks_at)
    at_hi = [arena.put(f"attn_t_hi{i}", [P, KT, P], F32R) for i in range(2)]
    at_lo = [arena.put(f"attn_t_lo{i}", [P, KT, P], F32R) for i in range(2)]

    s = nc.alloc_semaphore
    ones_set = s("ones_set")
    stack_loaded = [s(f"stack_loaded{i}") for i in range(SLOTS)]
    max_placed = [s(f"max_placed{i}") for i in range(SLOTS)]
    max_scored, max_part_ready, max_joined = s("max_scored"), s("max_part_ready"), s("max_joined")
    neg_hi_ready, neg_ready = s("neg_max_hi_ready"), s("neg_max_ready")
    max_turned, max_copied = s("max_turned"), s("max_copied")
    scored, exp_ready, weighed = s("scored"), s("exp_ready"), s("weighed")
    v_placed, out_copied = s("v_placed"), s("out_copied")
    inverted, normalized = s("sums_inverted"), s("group_normalized")
    wo_loaded, wo_hi_ready, wo_ready, bias_added = s("wo_loaded"), s("wo_hi_ready"), s("wo_ready"), s("bo_added")
    a_hi, a_lo = s("attn_hi_ready"), s("attn_lo_ready")
    projected, x_added = s("wo_projected"), s("wo_added")

    GROUPS = HEADS // SLOTS

    def over_heads(engine, step):
        for u in range(SLOTS):
            step(0, u, u)
        with engine.Fori(1, GROUPS - 1) as g:
            for u in range(SLOTS):
                step(g, u, g * SLOTS + u)
        for u in range(SLOTS):
            step(GROUPS - 1, u, (GROUPS - 1) * SLOTS + u)

    def is_const(h, low, high=HEADS):
        return isinstance(h, int) and not low <= h < high

    with nc.Block() as block:

        @block.sync
        def _(sp):
            parts_of = a["qk"].rearrange("w l b (h r) t -> w l (b h) r t", r=HD)

            def load(h, u):
                for row, half in enumerate((0, 0, 1)):
                    sp.dma_start(qs[u][row * HD:(row + 1) * HD, :].bitcast(F32),
                                 parts_of[0, half, h]).then_inc(stack_loaded[u], 16)
                for row, half in enumerate((0, 1, 0)):
                    sp.dma_start(ks[u][row * HD:(row + 1) * HD, :].bitcast(F32),
                                 parts_of[1, half, h]).then_inc(stack_loaded[u], 16)

            def place_max(h, u):
                sp.wait_ge(max_copied, h + 1)
                for half in range(2):
                    sp.dma_start(qs[u][ROWS + half:ROWS + half + 1, :].rearrange("a (t c) -> a t c", c=P).bitcast(F32),
                                 top_t[u % 2][half * QT:(half + 1) * QT, :].bitcast(F32)).then_inc(max_placed[u], 16)

            def step(g, u, h):
                if not is_const(h, 1, HEADS - SLOTS + 1):
                    sp.wait_ge(scored, N * h)
                    load(h - 1 + SLOTS, (u - 1) % SLOTS)
                if not is_const(h, 1, HEADS - 1):
                    place_max(h + 1, (u + 1) % SLOTS)
                if not is_const(h, 0, HEADS - 1):
                    dq.sync_load(sp, h + 1, u + 1)
                if not is_const(h, 1):
                    dq.sync_store(sp, h - 1)

            for u in range(SLOTS):
                load(u, u)
            sp.dma_start(wo_raw[:, :, :], a["wo"].rearrange("(k p) n -> p k n", p=P)).then_inc(wo_loaded, 16)
            dq.sync_load(sp, 0, 0)
            for u in range(AHEAD):
                place_max(u, u)
            over_heads(sp, step)
            dq.sync_store(sp, HEADS - 1)
            sp.wait_ge(dq.stored, 48 * HEADS)

        @block.gpsimd
        def _(pool):
            for i in range(SLOTS):
                pool.memset(ks[i][ROWS:ROWS + 2, :].bitcast(F32), 1.0).then_inc(ones_set, 1)
            pool.wait_ge(ones_set, SLOTS)
            for i in range(SLOTS):
                pool.memset(vs[i][:, :, HD:], 1.0).then_inc(ones_set, 1)
            pool.wait_ge(ones_set, 2 * SLOTS)
            dq.gpsimd_shifts(pool)

            def place_v(h, u):
                pool.tensor_copy(vs[u % SLOTS][:, :, 0:HD], m.v[:, h, :, :]).then_inc(v_placed, 1)

            def step(g, u, h):
                if not is_const(h, 0, HEADS - AHEAD):
                    need(pool, weighed, N * (h + AHEAD - SLOTS + 1))
                    place_v(h + AHEAD, u + AHEAD)
                dq.gpsimd_values(pool, h, u)
                if isinstance(h, int) and h >= HEADS - SLOTS:
                    for t in range(u * NT // SLOTS, (u + 1) * NT // SLOTS):
                        pool.tensor_tensor(m.x[:, t, :], m.x[:, t, :], m.bo[:, :], ALU.add).then_inc(bias_added, 1)

            for u in range(AHEAD):
                place_v(u, u)
            pool.wait_ge(wo_loaded, 16)
            pool.tensor_copy(wo_hi[:, :, :], wo_raw[:, :, :]).then_inc(wo_hi_ready, 1)
            pool.wait_ge(wo_hi_ready, 1)
            pool.tensor_tensor(wo_lo[:, :, :], wo_raw[:, :, :], wo_hi[:, :, :].bitcast(F32),
                               ALU.subtract).then_inc(wo_ready, 1)
            over_heads(pool, step)
            ln.gpsimd_rstd(pool, NCH)

        @block.tensor
        def _(pe):
            def max_unit(h, u, i):
                q, half, n = MAX_UNITS[i]
                need(pe, max_part_ready, N * h + i - 2)
                bank = m.bank[MAXB[i % 3]]
                diagonal = (q + 1) * P - half * CH == n
                last = pe.matmul(bank[:, 0:n], qs[u][0:ROWS, q * P:(q + 1) * P], ks[u][0:ROWS, half * CH:half * CH + n],
                                 start=True, stop=not diagonal)
                if diagonal:
                    last = pe.matmul(bank[:, n - P:n], m.ident16[:, :], m.mask_qk[:, :], start=False, stop=True)
                last.then_inc(max_scored, 1)

            def exp_unit(h, u, i):
                k, q0, n = EXP_UNITS[i]
                need(pe, exp_ready, N * h + i - 2)
                bank = m.bank[EXPB[i % 3]]
                diagonal = q0 == k * P
                last = pe.matmul(bank[:, 0:n], ks[u][0:ROWS + 2, k * P:(k + 1) * P], qs[u][0:ROWS + 2, q0:q0 + n],
                                 start=True, stop=not diagonal)
                if diagonal:
                    last = pe.matmul(bank[:, 0:P], m.ident16[:, :], m.mask_kq[:, :], start=False, stop=True)
                last.then_inc(scored, 1)

            def value_unit(h, u, i):
                k, q0, n = EXP_UNITS[i]
                c = q0 // CH
                if i == 0:
                    pe.wait_ge(v_placed, h + 1)
                if k == 0:
                    need(pe, out_copied, 4 * h - 2 + 2 * c)
                pe.wait_ge(exp_ready, N * h + i + 1)
                pe.matmul(m.bank[OUTB[c]][0:2 * HD, q0 - c * CH:q0 - c * CH + n], vs[u][:, k, :], probs[i % EXPS][:, 0:n],
                          start=(k == 0), stop=(k == (c + 1) * TPC - 1)).then_inc(weighed, 1)

            def turn_max(h):
                pe.wait_ge(neg_ready, h + 1)
                need(pe, max_copied, h)
                pe.matmul(m.bank[TURNED[0]][TURNED[1], 0:P], top[:, :, :].rearrange("p a q -> p (a q)"), m.ident[:, :],
                          start=True, stop=True).then_inc(max_turned, 1)

            def step(g, u, h):
                ahead = (u + AHEAD) % SLOTS
                for i in range(N):
                    if not is_const(h, 0, HEADS - AHEAD):
                        if i == 0:
                            pe.wait_ge(stack_loaded[ahead], 96 * (g + 1 + (u + AHEAD) // SLOTS))
                        max_unit(h + AHEAD, ahead, i)
                    if i == 0:
                        pe.wait_ge(max_placed[u], 32 * (g + 1))
                    exp_unit(h, u, i)
                    if i >= LAG:
                        value_unit(h, u, i - LAG)
                    elif not is_const(h, 1):
                        value_unit(h - 1, (u - 1) % SLOTS, N - LAG + i)
                    if i == 3 and not is_const(h, 1, HEADS - 1):
                        turn_max(h + 1)

            pe.wait_ge(ones_set, 2 * SLOTS)
            for u in range(AHEAD):
                pe.wait_ge(stack_loaded[u], 96)
                for i in range(N):
                    max_unit(u, u, i)
                turn_max(u)
            over_heads(pe, step)
            for i in range(N - LAG, N):
                value_unit(HEADS - 1, SLOTS - 1, i)

            pe.wait_ge(wo_ready, 1)
            for t in range(NT):
                pe.wait_ge(a_lo, t + 1)
                need(pe, x_added, t - 2)
                product3(pe, m.bank[EXPB[t % 3]][:, :],
                         [(at_hi[t % 2][:, k, :], at_lo[t % 2][:, k, :], wo_hi[:, k, :], wo_lo[:, k, :])
                          for k in range(KT)]).then_inc(projected, 1)
                if LN_TURN <= t < LN_TURN + TPC:
                    ln.tensor_turn(pe, NCH, t - LN_TURN)

        @block.scalar
        def _(act):
            def copy_max(h, u):
                act.wait_ge(max_turned, h + 1)
                act.activation(top_t[u % 2][:, :], m.bank[TURNED[0]][TURNED[1], 0:P], ACT.Copy).then_inc(max_copied, 1)

            def copy_out(g, u, h, c):
                act.wait_ge(weighed, N * h + (N if c else LAST0 + 1))
                if u == 0:
                    need(act, normalized, PIECES * g - (0 if c else PIECES // 2))
                rows, cols = slice(u * HD, (u + 1) * HD), slice(c * CH, (c + 1) * CH)
                act.activation(out_t[rows, cols], m.bank[OUTB[c]][0:HD, :], ACT.Copy).then_inc(out_copied, 1)
                act.activation(sums_t[rows, cols], m.bank[OUTB[c]][HD:2 * HD, :], ACT.Copy).then_inc(out_copied, 1)

            def step(g, u, h):
                for i in range(N):
                    if i == LAST0 + LAG + 2:
                        copy_out(g, u, h, 0)
                    if i == 3 and not is_const(h, 1):
                        copy_out(*((g, u - 1) if u else (g - 1, SLOTS - 1)), h - 1, 1)
                    if i == 5 and not is_const(h, 1):
                        dq.scalar_hi(act, h - 1)
                    k, q0, n = EXP_UNITS[i]
                    act.wait_ge(scored, N * h + i + 1)
                    need(act, weighed, N * h + i - EXPS + 1)
                    act.activation(probs[i % EXPS][:, 0:n], m.bank[EXPB[i % 3]][:, 0:n], ACT.Exp,
                                   scale=scale).then_inc(exp_ready, 1)
                    if i == 4 and not is_const(h, 1, HEADS - 1):
                        act.wait_ge(max_placed[(u - 1) % SLOTS], 32 * (g + (1 if u else 0)))
                        copy_max(h + 1, u + 1)

            for u in range(AHEAD):
                copy_max(u, u)
            over_heads(act, step)
            for t in range(NT):
                if t == 2:
                    copy_out(GROUPS - 1, SLOTS - 1, HEADS - 1, 1)
                    dq.scalar_hi(act, HEADS - 1)
                b, q = t // QT, t % QT
                act.wait_ge(normalized, PIECES * (b + 1) * KT)
                need(act, projected, t - 1)
                act.activation(at_hi[t % 2][:, :, :], m.attn[:, b * KT:(b + 1) * KT, q * P:(q + 1) * P],
                               ACT.Copy).then_inc(a_hi, 1)
                if LN_TURN + 2 <= t < LN_TURN + 2 + TPC:
                    ln.scalar_hi(act, NCH, t - LN_TURN - 2)

        @block.vector
        def _(dve):
            def max_part(h, u, i):
                q, half, n = MAX_UNITS[i]
                dve.wait_ge(max_scored, N * h + i + 1)
                dve.tensor_reduce(parts[u % 2][:, half, q:q + 1], m.bank[MAXB[i % 3]][:, 0:n], AX.X,
                                  ALU.max).then_inc(max_part_ready, 1)

            def join_max(h, u):
                both = parts[u % 2]
                dve.wait_ge(max_part_ready, N * (h + 1))
                dve.tensor_tensor(both[:, 0, TPC:], both[:, 0, TPC:], both[:, 1, TPC:], ALU.max).then_inc(max_joined, 1)
                need(dve, max_turned, h)
                dve.wait_ge(max_joined, h + 1)
                dve.tensor_scalar(top[:, 0, :].bitcast(F32R), both[:, 0, :], -1.0, None, ALU.mult).then_inc(neg_hi_ready, 1)
                dve.wait_ge(neg_hi_ready, h + 1)
                dve.scalar_tensor_tensor(out=top[:, 1, :].bitcast(F32R), in0=both[:, 0, :], scalar=-1.0, in1=top[:, 0, :],
                                         op0=ALU.mult, op1=ALU.subtract).then_inc(neg_ready, 1)

            def normalize(g, piece):
                cols = slice(piece * S // PIECES, (piece + 1) * S // PIECES)
                if piece == 0:
                    dve.wait_ge(out_copied, 4 * SLOTS * (g + 1) - 2)
                if piece == PIECES // 2:
                    dve.wait_ge(out_copied, 4 * SLOTS * (g + 1))
                dve.reciprocal(sums_t[:, cols], sums_t[:, cols]).then_inc(inverted, 1)
                dve.wait_ge(inverted, PIECES * g + piece + 1)
                dve.tensor_tensor(m.attn[:, g, cols], out_t[:, cols], sums_t[:, cols], ALU.mult).then_inc(normalized, 1)

            def step(g, u, h):
                for i in range(N):
                    if not is_const(h, 0, HEADS - AHEAD):
                        max_part(h + AHEAD, u, i)
                    if (u, i) in PIECE_AT and not is_const(h, SLOTS - 1):
                        normalize(g if u == SLOTS - 1 else g - 1, PIECE_AT[u, i])
                    if i == 7 and not is_const(h, 1):
                        dq.vector_lo(dve, h - 1)
                    if i == NIBBLES_AT:
                        dq.vector_nibbles(dve, g, u, h)
                    if i == NIBBLES_AT + 1:
                        dq.vector_signs(dve, u)
                    if i == NIBBLES_AT + 2:
                        dq.vector_codes(dve, h)
                if not is_const(h, 0, HEADS - AHEAD):
                    join_max(h + AHEAD, u)

            dq.vector_shifts(dve)
            for u in range(AHEAD):
                for i in range(N):
                    max_part(u, u, i)
                join_max(u, u)
            over_heads(dve, step)
            def split_attn(t):
                dve.wait_ge(a_hi, t + 1)
                b, q = t // QT, t % QT
                dve.tensor_tensor(at_lo[t % 2][:, :, :], m.attn[:, b * KT:(b + 1) * KT, q * P:(q + 1) * P],
                                  at_hi[t % 2][:, :, :].bitcast(F32), ALU.subtract).then_inc(a_lo, 1)

            for t in range(2):
                split_attn(t)
            for piece in range(2, PIECES):
                normalize(GROUPS - 1, piece)
            dq.vector_lo(dve, HEADS - 1)
            dve.wait_ge(bias_added, NT)
            for t in range(NT):
                dve.wait_ge(projected, t + 1)
                dve.tensor_tensor(m.x[:, t, :], m.x[:, t, :], m.bank[EXPB[t % 3]][:, :],
                                  ALU.add).then_inc(x_added, 1)
                if t + 2 < NT:
                    split_attn(t + 2)
                if t == TPC:
                    dve.wait_ge(x_added, TPC)
                    ln.vector_stats(dve, NCH)
                if t == TPC + 2:
                    ln.vector_normalize(dve, NCH)
                if LN_TURN + 1 <= t < LN_TURN + 1 + TPC:
                    ln.vector_lo(dve, NCH, t - LN_TURN - 1)


def ffn_phase(nc, m, a):
    arena = Arena(nc, m.base)
    gu_hi = arena.put("gu_hi", [P, KT, 2 * I0], F32R)
    gu_lo = arena.put("gu_lo", [P, KT, 2 * I0], F32R)
    down_hi = arena.put("down_hi", [P, G0, D], F32R)
    down_lo = arena.put("down_lo", [P, G0, D], F32R)
    ln = LayerNorm(nc, m, arena, "ln2", buffers=1, first=1, nibbles=range(1, NCH))
    hidden = [arena.put(f"hidden{i}", [P, CH], F32) for i in range(2)]
    square = arena.put("y_square", [P, D], F32)
    square_sum = arena.put("y_square_sum", [P, TPC], F32)
    y_rms = arena.put("y_inverse_rms", [P, TPC], F32)
    root = InverseRoot(nc, arena, "rms", TPC)
    hidden_hi = [arena.put("hidden_hi0", [P, CH], F32R)]
    hidden_lo = [arena.put("hidden_lo0", [P, CH], F32R)]
    assert arena.at <= SBUF_END - 4 * (TPC * D + 2 * KT * CH)
    arena = Arena(nc, m.attention_rows)
    hidden_hi.append(arena.put("hidden_hi1", [P, CH], F32R))
    hidden_lo.append(arena.put("hidden_lo1", [P, CH], F32R))
    GATEB, UPB, DOWNB = (0, 1), (2, 3), (4, 5, 6, 7)

    s = nc.alloc_semaphore
    PIECES = (0, 1, 4, 8, G0)
    gu_loaded = [s(f"gu_piece_loaded{i}") for i in range(len(PIECES) - 1)]
    down_loaded = [s(f"down_piece_loaded{i}") for i in range(len(PIECES) - 1)]
    gate_done, up_done = s("gate_done"), s("up_done")
    silu_ready, hidden_ready = s("silu_ready"), s("hidden_ready")
    hi_ready, lo_ready, slot_used = s("hidden_hi_ready"), s("hidden_lo_ready"), s("hidden_slot_used")
    y_done, squared, rms_ready, y_added = s("y_done"), s("y_squared"), s("rms_ready"), s("y_added")

    with nc.Block() as block:

        @block.sync
        def _(sp):
            for i in range(len(PIECES) - 1):
                for half in range(2):
                    cols = slice(half * I0 + PIECES[i] * P, half * I0 + PIECES[i + 1] * P)
                    for n, w in ((1, gu_hi), (2, gu_lo)):
                        src = a["fp4_out"][n, :, 0:GU_COLS].rearrange("p (k n) -> p k n", k=KT)
                        sp.dma_start(w[:, :, cols].bitcast(F32), src[:, :, cols]).then_inc(gu_loaded[i], 16)
                groups = slice(PIECES[i], PIECES[i + 1])
                for n, w in ((1, down_hi), (2, down_lo)):
                    src = a["fp4_out"][n, :, GU_COLS:].rearrange("p (g n) -> p g n", g=G0)
                    sp.dma_start(w[:, groups, :].bitcast(F32), src[:, groups, :]).then_inc(down_loaded[i], 16)

        @block.gpsimd
        def _(pool):
            for c in range(NCH):
                ln.gpsimd_rstd(pool, c + 1)
                pool.wait_ge(root.ready, c + 1)
                need(pool, y_added, TPC * c)
                root.gpsimd_refine(pool, y_rms[:, :], rms_ready)

        @block.tensor
        def _(pe):
            def down(c, g):
                n = G0 * c + g
                pe.wait_ge(lo_ready, n + 1)
                if c == 0 and g in PIECES:
                    pe.wait_ge(down_loaded[PIECES.index(g)], 32)
                if g == 0:
                    need(pe, y_added, TPC * c)
                for j in range(TPC):
                    tok = slice(j * P, (j + 1) * P)
                    last = product3(pe, m.bank[DOWNB[j]][:, :],
                                    [(hidden_hi[n % 2][:, tok], hidden_lo[n % 2][:, tok], down_hi[:, g, :], down_lo[:, g, :])],
                                    start=g == 0, stop=g == G0 - 1)
                    if g == G0 - 1:
                        last.then_inc(y_done, 1)
                if g < G0 - 1:
                    last.then_inc(slot_used, 1)

            for c in range(NCH):
                ln.wait_lo(pe, c)
                hi, lo = ln.hi[0], ln.lo[0]
                for g in range(G0):
                    n = G0 * c + g
                    need(pe, hidden_ready, n - 1)
                    if c == 0 and g in PIECES:
                        pe.wait_ge(gu_loaded[PIECES.index(g)], 64)
                    for half, bank, done in ((0, GATEB, gate_done), (1, UPB, up_done)):
                        w = slice(half * I0 + g * P, half * I0 + (g + 1) * P)
                        product3(pe, m.bank[bank[n % 2]][:, :],
                                 [(gu_hi[:, k, w], gu_lo[:, k, w], hi[:, k, :], lo[:, k, :])
                                  for k in range(KT)]).then_inc(done, 1)
                    if g >= 1:
                        down(c, g - 1)
                pe.wait_ge(silu_ready, G0 * (c + 1))
                for j in range(TPC):
                    if j == 2:
                        down(c, G0 - 1)
                    ln.tensor_turn(pe, c + 1, j)

        @block.scalar
        def _(act):
            def to_hi(c, g):
                n = G0 * c + g
                act.wait_ge(hidden_ready, n + 1)
                if n >= 2:
                    c2, g2 = (n - 2) // G0, (n - 2) % G0
                    if g2 == G0 - 1:
                        act.wait_ge(y_done, TPC * (c2 + 1))
                    else:
                        act.wait_ge(slot_used, (G0 - 1) * c2 + g2 + 1)
                act.activation(hidden_hi[n % 2][:, :], hidden[n % 2][:, :], ACT.Copy).then_inc(hi_ready, 1)

            for c in range(NCH):
                for g in range(G0):
                    n = G0 * c + g
                    if g >= 1:
                        to_hi(c, g - 1)
                    act.wait_ge(gate_done, n + 1)
                    need(act, lo_ready, n - 1)
                    act.activation(hidden[n % 2][:, :], m.bank[GATEB[n % 2]][:, :], ACT.Silu).then_inc(silu_ready, 1)
                to_hi(c, G0 - 1)
                act.wait_ge(up_done, G0 * (c + 1))
                last = c + 1 == NCH
                for j in range(2 if last else TPC):
                    ln.scalar_hi(act, c + 1, j)
                need(act, root.v_ready, c)
                for j in range(TPC):
                    t = TPC * c + j
                    act.wait_ge(y_done, t + 1)
                    need(act, squared, t)
                    act.activation(square[:, :], m.bank[DOWNB[j]][:, :], ACT.Square,
                                   accum_out=square_sum[:, j:j + 1]).then_inc(squared, 1)
                for j in range(2 if last else TPC, TPC):
                    ln.scalar_hi(act, c + 1, j)

        @block.vector
        def _(dve):
            def to_lo(c, g):
                n = G0 * c + g
                dve.wait_ge(hi_ready, n + 1)
                dve.tensor_tensor(hidden_lo[n % 2][:, :], hidden[n % 2][:, :], hidden_hi[n % 2][:, :].bitcast(F32),
                                  ALU.subtract).then_inc(lo_ready, 1)

            def guess_rms(c):
                dve.wait_ge(squared, TPC * (c + 1))
                need(dve, rms_ready, c)
                root.vector_guess(dve, square_sum[:, :], 1.0 / D, RMS_EPS)

            def add_y(c):
                dve.wait_ge(rms_ready, c + 1)
                for j in range(TPC):
                    t = TPC * c + j
                    dve.scalar_tensor_tensor(out=m.x[:, t, :], in0=m.bank[DOWNB[j]][:, :], scalar=y_rms[:, j:j + 1],
                                             in1=m.x[:, t, :], op0=ALU.mult, op1=ALU.add).then_inc(y_added, 1)

            for c in range(NCH):
                for g in range(G0):
                    n = G0 * c + g
                    if g >= 1:
                        to_lo(c, g - 1)
                    if c >= 1 and g == 0:
                        guess_rms(c - 1)
                    if c >= 1 and g == 1:
                        add_y(c - 1)
                    if g == 4:
                        if c + 1 == NCH:
                            dve.wait_ge(y_added, TPC)
                        ln.vector_stats(dve, c + 1)
                    if g == 7:
                        ln.vector_normalize(dve, c + 1)
                    dve.wait_ge(silu_ready, n + 1)
                    dve.wait_ge(up_done, n + 1)
                    dve.tensor_tensor(hidden[n % 2][:, :], hidden[n % 2][:, :], m.bank[UPB[n % 2]][:, :],
                                      ALU.mult).then_inc(hidden_ready, 1)
                to_lo(c, G0 - 1)
                for j in range(TPC):
                    if c + 1 == NCH and j == 2:
                        guess_rms(c)
                    ln.vector_lo(dve, c + 1, j)
            add_y(NCH - 1)


def recurrence_phase(nc, m, a):
    arena = Arena(nc, m.base)
    parts = {}
    for name in ("w_in", "w_out"):
        parts[name] = [arena.put(f"{name}_{p}", [P, KT, D], dt) for p, dt in (("raw", F32), ("hi", F32R), ("lo", F32R))]
    ln = LayerNorm(nc, m, arena, "ln3", first=1)
    decay = arena.put("decay_cols", [P, 4, KT], F32)
    drive = [arena.put(f"drive{i}", [P, CH], F32) for i in range(2)]
    state = [arena.put(f"state{i}", [P, KT, CH], F32) for i in range(2)]
    st_hi = [arena.put(f"state_hi{i}", [P, KT, CH], F32R) for i in range(2)]
    st_lo = [arena.put(f"state_lo{i}", [P, KT, CH], F32R) for i in range(2)]
    INB, OUTB = (2, 3, 4), (5, 6, 7)

    s = nc.alloc_semaphore
    w_in_loaded = [s(f"w_in_loaded{k}") for k in range(KT)]
    w_out_loaded = s("w_out_loaded")
    w_hi_ready = {n: s(f"{n}_hi_ready") for n in parts}
    w_ready = {n: s(f"{n}_ready") for n in parts}
    decay_loaded, decay_step = s("decay_loaded"), s("decay_step")
    in_done, drive_ready, scanned = s("in_done"), s("drive_ready"), s("scanned")
    st_hi_ready, st_lo_ready = s("state_hi_ready"), s("state_lo_ready")
    bias_added, out_done, x_added = s("b1_added"), s("out_done"), s("rec_added")

    with nc.Block() as block:

        @block.sync
        def _(sp):
            for k in range(KT):
                sp.dma_start(parts["w_in"][0][:, k, :], a["w_in"][k * P:(k + 1) * P, :]).then_inc(w_in_loaded[k], 16)
            with nc.allow_non_contiguous_dma("four small decay columns"):
                sp.dma_start(decay[:, 0, :], a["decay"].rearrange("(k p) -> p k", p=P)).then_inc(decay_loaded, 16)
            sp.dma_start(parts["w_out"][0][:, :, :], a["w_out"].rearrange("(k p) n -> p k n", p=P)).then_inc(w_out_loaded, 16)

        @block.gpsimd
        def _(pool):
            ln.gpsimd_rstd(pool, 1)
            raw, hi, lo = parts["w_out"]
            pool.wait_ge(w_hi_ready["w_out"], 1)
            pool.tensor_tensor(lo[:, :, :], raw[:, :, :], hi[:, :, :].bitcast(F32), ALU.subtract).then_inc(w_ready["w_out"], 1)
            for c in range(NCH):
                ln.wait_xn(pool, c)
                if c >= 1:
                    ln.gpsimd_rstd(pool, c + 1)
                for t in range(TPC * c, TPC * (c + 1)):
                    pool.tensor_tensor(m.x[:, t, :], m.x[:, t, :], m.b1[:, :], ALU.add).then_inc(bias_added, 1)

        @block.tensor
        def _(pe):
            def project_in(c):
                hi, lo = ln.hi[c % 2], ln.lo[c % 2]
                ln.wait_lo(pe, c)
                for e in range(KT):
                    n = KT * c + e
                    need(pe, drive_ready, n - 2)
                    w = slice(e * P, (e + 1) * P)
                    _, w_hi, w_lo = parts["w_in"]
                    product3(pe, m.bank[INB[n % 3]][:, :],
                             [(w_hi[:, k, w], w_lo[:, k, w], hi[:, k, :], lo[:, k, :]) for k in range(KT)]).then_inc(in_done, 1)
                    if c + 1 < NCH:
                        ln.tensor_turn(pe, c + 1, e)

            pe.wait_ge(w_ready["w_in"], KT)
            project_in(0)
            pe.wait_ge(w_ready["w_out"], 1)
            for c in range(NCH):
                if c + 1 < NCH:
                    project_in(c + 1)
                pe.wait_ge(st_lo_ready, KT * (c + 1))
                for j in range(TPC):
                    if c + 1 == NCH:
                        ln.tensor_turn(pe, NCH, j)
                    t = TPC * c + j
                    need(pe, x_added, t - 2)
                    tok = slice(j * P, (j + 1) * P)
                    _, w_hi, w_lo = parts["w_out"]
                    product3(pe, m.bank[OUTB[t % 3]][:, :],
                             [(st_hi[c % 2][:, k, tok], st_lo[c % 2][:, k, tok], w_hi[:, k, :], w_lo[:, k, :]) for k in range(KT)]).then_inc(out_done, 1)

        @block.scalar
        def _(act):
            raw, hi, _ = parts["w_in"]
            for k in range(KT):
                act.wait_ge(w_in_loaded[k], 16)
                act.activation(hi[:, k, :], raw[:, k, :], ACT.Copy).then_inc(w_hi_ready["w_in"], 1)
            act.wait_ge(decay_loaded, 16)
            act.activation(decay[:, 1, :], decay[:, 0, :], ACT.Exp, scale=-1.0).then_inc(decay_step, 1)
            raw, hi, _ = parts["w_out"]
            act.wait_ge(w_out_loaded, 16)
            act.activation(hi[:, :, :], raw[:, :, :], ACT.Copy).then_inc(w_hi_ready["w_out"], 1)
            act.wait_ge(decay_step, 4)
            for c in range(NCH):
                for e in range(KT):
                    n = KT * c + e
                    act.wait_ge(in_done, n + 1)
                    need(act, scanned, n - 1)
                    act.activation(drive[n % 2][:, :], m.bank[INB[n % 3]][:, :], ACT.Copy,
                                   scale=decay[:, 3, e:e + 1]).then_inc(drive_ready, 1)
                    if c + 1 < NCH:
                        ln.scalar_hi(act, c + 1, e)
                    act.wait_ge(scanned, n + 1)
                    if c >= 2 and e == 0:
                        act.wait_ge(out_done, TPC * (c - 1))
                    act.activation(st_hi[c % 2][:, e, :], state[c % 2][:, e, :], ACT.Copy).then_inc(st_hi_ready, 1)
            for j in range(TPC):
                ln.scalar_hi(act, NCH, j)

        @block.vector
        def _(dve):
            ln.vector_stats(dve, 1)
            raw, hi, lo = parts["w_in"]
            for k in range(KT):
                dve.wait_ge(w_hi_ready["w_in"], k + 1)
                dve.tensor_tensor(lo[:, k, :], raw[:, k, :], hi[:, k, :].bitcast(F32), ALU.subtract).then_inc(w_ready["w_in"], 1)
            ln.vector_normalize(dve, 1)
            ln.vector_stats(dve, 2)
            dve.wait_ge(decay_step, 1)
            dve.tensor_scalar(decay[:, 1, :], decay[:, 1, :], 1.0, None, ALU.add).then_inc(decay_step, 1)
            dve.wait_ge(decay_step, 2)
            dve.reciprocal(decay[:, 2, :], decay[:, 1, :]).then_inc(decay_step, 1)
            dve.wait_ge(decay_step, 3)
            dve.tensor_scalar(decay[:, 3, :], decay[:, 2, :], -1.0, 1.0, ALU.mult, ALU.add).then_inc(decay_step, 1)

            def add_out(t):
                dve.wait_ge(out_done, t + 1)
                dve.tensor_tensor(m.x[:, t, :], m.x[:, t, :], m.bank[OUTB[t % 3]][:, :], ALU.add).then_inc(x_added, 1)

            for c in range(NCH):
                for e in range(KT):
                    n = KT * c + e
                    dve.wait_ge(drive_ready, n + 1)
                    carry = 0.0 if c % (S // CH) == 0 else state[(c - 1) % 2][:, e, CH - 1:CH]
                    dve.tensor_tensor_scan(state[c % 2][:, e, :], decay[:, 2, e:e + 1].to_broadcast([P, CH]),
                                           drive[n % 2][:, :], carry, ALU.mult, ALU.add).then_inc(scanned, 1)
                    if c + 1 < NCH:
                        ln.vector_lo(dve, c + 1, e)
                    dve.wait_ge(st_hi_ready, n + 1)
                    dve.tensor_tensor(st_lo[c % 2][:, e, :], state[c % 2][:, e, :], st_hi[c % 2][:, e, :].bitcast(F32),
                                      ALU.subtract).then_inc(st_lo_ready, 1)
                    if c + 2 <= NCH:
                        ln.vector_normalize_tile(dve, c + 2, e)
                if c >= 1:
                    dve.wait_ge(bias_added, TPC * c)
                    for j in range(TPC):
                        add_out(TPC * (c - 1) + j)
                if c + 3 == NCH:
                    dve.wait_ge(x_added, TPC)
                if c + 3 <= NCH:
                    ln.vector_stats(dve, c + 3)
            dve.wait_ge(bias_added, NT)
            for j in range(TPC):
                ln.vector_lo(dve, NCH, j)
                add_out(NT - TPC + j)


PREFETCHED = 2
WEIGHT_LOADS = 4
DOWN_FULL = F // P


def experts_weights(arena, sets):
    return [(arena.put(f"w_gate{i}", [P, KT, F], F32), arena.put(f"w_up{i}", [P, KT, F], F32),
             arena.put(f"w_down{i}", [P, DOWN_FULL + 1, D], F32)) for i in sets]


def load_gate_up(sp, a, weights, e, loaded):
    for w, name in zip(weights, ("w_gate", "w_up")):
        src = a[name][bass.ds(e, 1)].rearrange("o (p k) n -> p (o k) n", p=P)
        sp.dma_start(w[:, :, :], src).then_inc(loaded, 16)


def load_down(sp, a, weights, e, loaded):
    w, src = weights[2], a["w_down"][bass.ds(e, 1)]
    sp.dma_start(w[:, 0:DOWN_FULL, :], src[:, 0:DOWN_FULL * P, :].rearrange("o (k p) n -> p (o k) n", p=P)).then_inc(loaded, 16)
    sp.dma_start(w[0:F - DOWN_FULL * P, DOWN_FULL, :], src[:, DOWN_FULL * P:, :].rearrange("o p n -> p (o n)")).then_inc(loaded, 16)


def router_phase(nc, m, a):
    arena = Arena(nc, m.base)
    m.slot_rows = arena.put("slot_rows", [P, E], U32)
    m.after_slots = arena.at
    GS = (FS + P - 1) // P
    rows = [min(P, FS - g * P) for g in range(GS)]
    w_hi = {n: arena.put(f"{n}_hi", [P, KT, FS], F32R) for n in ("sh_gate", "sh_up")}
    w_lo = {n: arena.put(f"{n}_lo", [P, KT, FS], F32R) for n in ("sh_gate", "sh_up")}
    w_raw = arena.put("sh_up_raw", [P, KT, FS], F32)
    gw_raw = arena.put("gate_w_raw", [P, KT, E], F32)
    gw_hi = arena.put("gate_w_hi", [P, KT, E], F32R)
    gw_lo = arena.put("gate_w_lo", [P, KT, E], F32R)
    stage = arena.put("sh_stage", [P, GS, D], F32)
    down_hi = arena.put("sh_down_hi", [P, GS, D], F32R)
    down_lo = arena.put("sh_down_lo", [P, GS, D], F32R)
    ln = LayerNorm(nc, m, arena, "ln4", buffers=1, first=1)
    hidden = [arena.put(f"sh_hidden{i}", [P, CH], F32) for i in range(2)]
    hidden_hi = arena.put("sh_hidden_hi", [P, GS, CH], F32R)
    hidden_lo = arena.put("sh_hidden_lo", [P, GS, CH], F32R)
    silu = [arena.put(f"sh_silu{i}", [P, CH], F32) for i in range(2)]
    logits_e = arena.put("logits_e", [E, CH], F32)
    logits = arena.put("logits", [P, TPC, E], F32)
    top = arena.put("logit_max", [P, TPC], F32)
    total = arena.put("exp_sum", [P, TPC], F32)
    scores = arena.put("scores", [P, TPC, E + 2], F32)
    best = arena.put("best", [P, TPC, 8], F32)
    marked = arena.put("marked", [P, TPC, E + 2], F32)
    keys = arena.put("keys", [P, TPC, E], F32)
    ranks = [arena.put(f"ranks{i}", [E, CAP + CH], F32) for i in range(2)]
    kept = arena.put("kept", [E, CAP], F32)
    iota_i = arena.put("key_iota", [P, NT], I32)
    key_of = arena.put("key_of_token", [P, NT], F32)
    slot_i = arena.put("slot_iota", [P, 1], I32)
    slot_f = arena.put("slot_number", [P, 1], F32)
    empty = arena.put("slot_empty", [P, E], F32)
    rows_f = arena.put("slot_rows_f", [P, E], F32)
    zero = arena.put("zero_rows", [P, XS], F32)
    GATEB, UPB, DOWNB = (2, 3), (4, 5), (6, 7)
    EB, TB = DOWNB
    SENTINEL = 2.0
    ROUNDS = CAP // 8

    s = nc.alloc_semaphore
    w_loaded = {n: s(f"{n}_loaded") for n in ("gate_w", "sh_gate", "sh_up", "sh_down")}
    w_hi_ready = {n: s(f"{n}_hi_ready") for n in ("gate_w", "sh_gate", "sh_up")}
    w_ready = {n: s(f"{n}_ready") for n in ("gate_w", "sh_gate", "sh_up")}
    iota_set, zero_set, consts = s("router_iota_set"), s("zero_rows_set"), s("router_consts_ready")
    xn_stored, scores_stored, out_stored = s("xn_stored"), s("scores_stored"), s("out_stored")
    logits_done, logits_copied, logits_turned = s("logits_done"), s("logits_copied"), s("logits_turned")
    max_ready, shifted, exp_ready, sum_ready = s("logit_max_ready"), s("logits_shifted"), s("router_exp_ready"), s("exp_sum_ready")
    inverse_ready, scores_ready = s("exp_inverse_ready"), s("scores_ready")
    best_ready, best_set, marks_ready, keys_ready = s("best_ready"), s("best_set"), s("marks_ready"), s("keys_ready")
    keys_turned, keys_copied, rank_step, kept_moved = s("keys_turned"), s("keys_copied"), s("rank_step"), s("kept_moved")
    kept_turned, empty_ready, rows_ready, slots_ready = s("kept_turned"), s("slot_empty_ready"), s("slot_rows_f_ready"), s("slots_ready")
    gate_done, up_done, silu_ready, hidden_ready = s("sh_gate_done"), s("sh_up_done"), s("sh_silu_ready"), s("sh_hidden_ready")
    y_done, y_added = s("sh_y_done"), s("sh_y_added")
    gate_raw = stage[:, :, :].rearrange("p g n -> p (g n)")[:, 0:KT * FS].rearrange("p (k n) -> p k n", k=KT)
    raws = {"gate_w": gw_raw[:, :, :], "sh_gate": gate_raw, "sh_up": w_raw[:, :, :]}
    down_hi_ready, down_ready = s("sh_down_hi_ready"), s("sh_down_ready")
    hidden_hi_ready, hidden_lo_ready = s("sh_hidden_hi_ready"), s("sh_hidden_lo_ready")
    TILES = ((slice(0, P), slice(0, GS - 1)), (slice(0, rows[GS - 1]), slice(GS - 1, GS)))
    w_rest_ready = {n: s(f"{n}_rest_ready") for n in ("sh_gate", "sh_up")}
    parts = {"gate_w": (gw_hi, gw_lo), "sh_gate": (w_hi["sh_gate"], w_lo["sh_gate"]), "sh_up": (w_hi["sh_up"], w_lo["sh_up"])}
    xn_rows = a["xs"][0:T, 0:D].rearrange("(t p) d -> p t d", p=P)
    score_rows = a["xs"][0:T, D:XS].rearrange("(t p) e -> p t e", p=P)
    out_rows = a["out"][0:T, :].rearrange("(t p) d -> p t d", p=P)

    CUT = min(GS // 2 * P, FS)
    halves = [slice(0, CUT), slice(CUT, FS)]
    assert arena.at <= SBUF_END - 4 * (TPC * D + 2 * KT * CH)
    m.experts = experts_weights(Arena(nc, m.after_slots), range(PREFETCHED))
    prefetched = s("experts_prefetched")

    with nc.Block() as block:

        @block.sync
        def _(sp):
            for name in ("gate_w", "sh_gate", "sh_up"):
                sp.dma_start(raws[name], a[name].rearrange("(k p) n -> p k n", p=P)).then_inc(w_loaded[name], 16)
            sp.wait_ge(w_ready["sh_gate"], 1)
            sp.wait_ge(w_rest_ready["sh_gate"], 1)
            full = GS - 1
            sp.dma_start(stage[:, 0:full, :], a["sh_down"][0:full * P, :].rearrange("(g p) n -> p g n", p=P)).then_inc(w_loaded["sh_down"], 16)
            sp.dma_start(stage[0:rows[full], full, :], a["sh_down"][full * P:FS, :]).then_inc(w_loaded["sh_down"], 16)
            sp.wait_ge(zero_set, 1)
            sp.dma_start(a["xs"][T:T + P, :], zero[:, :]).then_inc(xn_stored, 16)
            sp.dma_start(a["out"][T:T + P, :], zero[:, 0:D]).then_inc(out_stored, 16)
            for c in range(NCH):
                tiles = slice(TPC * c, TPC * (c + 1))
                ln.wait_xn(sp, c)
                sp.dma_start(xn_rows[:, tiles, :], ln.xn[:, :, :]).then_inc(xn_stored, 16)
                sp.wait_ge(scores_ready, c + 1)
                sp.dma_start(score_rows[:, tiles, :], scores[:, :, 0:E]).then_inc(scores_stored, 16)
                if c + 1 == NCH:
                    sp.wait_ge(up_done, GS * NCH)
                    for e in range(PREFETCHED):
                        load_gate_up(sp, a, m.experts[e], e, prefetched)
                        load_down(sp, a, m.experts[e], e, prefetched)
                for t in range(TPC * c, TPC * (c + 1)):
                    sp.wait_ge(y_added, t + 1)
                    sp.dma_start(out_rows[:, t, :], m.x[:, t, :]).then_inc(out_stored, 16)
            sp.wait_ge(xn_stored, 16 * (NCH + 1))
            sp.wait_ge(prefetched, 16 * WEIGHT_LOADS * PREFETCHED)
            sp.wait_ge(scores_stored, 16 * NCH)
            sp.wait_ge(out_stored, 16 * (NT + 1))

        @block.gpsimd
        def _(pool):
            pool.memset(zero[:, :], 0.0).then_inc(zero_set, 1)
            pool.iota(iota_i[:, :], pattern=[[-P, NT]], base=T, channel_multiplier=-1).then_inc(iota_set, 1)
            pool.iota(slot_i[:, :], pattern=[[0, 1]], base=0, channel_multiplier=1).then_inc(iota_set, 1)
            for name in ("sh_gate", "sh_up"):
                hi, lo = parts[name]
                cols = halves[1]
                pool.wait_ge(w_hi_ready[name], 2)
                pool.tensor_tensor(lo[:, :, cols], raws[name][:, :, cols], hi[:, :, cols].bitcast(F32),
                                   ALU.subtract).then_inc(w_rest_ready[name], 1)
            pool.wait_ge(down_hi_ready, 2)
            for p, k in TILES:
                pool.tensor_tensor(down_lo[p, k, :], stage[p, k, :], down_hi[p, k, :].bitcast(F32),
                                   ALU.subtract).then_inc(down_ready, 1)
                pool.wait_ge(down_ready, 1)
            for c in range(NCH):
                for g, r in enumerate(rows):
                    n = GS * c + g
                    pool.wait_ge(hidden_hi_ready, n + 1)
                    need(pool, hidden_lo_ready, n)
                    pool.tensor_tensor(hidden_lo[0:r, g, :], hidden[n % 2][0:r, :], hidden_hi[0:r, g, :].bitcast(F32),
                                       ALU.subtract).then_inc(hidden_lo_ready, 1)
                    if g == 2 and c + 1 < NCH:
                        ln.gpsimd_rstd(pool, c + 1)

        @block.tensor
        def _(pe):
            def logits_of(c):
                ln.wait_lo(pe, c)
                need(pe, y_added, TPC * c - 1)
                product3(pe, m.bank[EB][0:E, :],
                         [(gw_hi[:, k, :], gw_lo[:, k, :], ln.hi[0][:, k, :], ln.lo[0][:, k, :])
                          for k in range(KT)]).then_inc(logits_done, 1)

            def turn_logits(c):
                pe.wait_ge(logits_copied, c + 1)
                need(pe, y_added, TPC * c)
                for j in range(TPC):
                    last = pe.transpose(m.bank[TB][:, j * E:(j + 1) * E], logits_e[:, j * P:(j + 1) * P], m.ident[0:E, 0:E])
                last.then_inc(logits_turned, 1)

            def turn_keys(c):
                pe.wait_ge(keys_ready, TPC * (c + 1))
                for j in range(TPC):
                    last = pe.transpose(m.bank[EB][0:E, j * P:(j + 1) * P], keys[:, j, :], m.ident[:, :])
                last.then_inc(keys_turned, 1)

            pe.wait_ge(w_ready["gate_w"], 1)
            for c in range(NCH):
                logits_of(c)
                hi, lo = ln.hi[0], ln.lo[0]
                for g in range(GS):
                    n, r = GS * c + g, rows[g]
                    need(pe, hidden_ready, n - 1)
                    for name, bank, done in (("sh_gate", GATEB, gate_done), ("sh_up", UPB, up_done)):
                        if c == 0 and g == 0:
                            pe.wait_ge(w_ready[name], 1)
                        if c == 0 and g * P == CUT:
                            pe.wait_ge(w_rest_ready[name], 1)
                        w = slice(g * P, g * P + r)
                        product3(pe, m.bank[bank[n % 2]][0:r, :],
                                 [(w_hi[name][:, k, w], w_lo[name][:, k, w], hi[:, k, :], lo[:, k, :])
                                  for k in range(KT)]).then_inc(done, 1)
                    if g == 0:
                        turn_logits(c)
                    if g == 3:
                        turn_keys(c)
                if c == 0:
                    pe.wait_ge(down_ready, 2)
                for j in range(TPC):
                    if c + 1 < NCH:
                        ln.tensor_turn(pe, c + 1, j)
                    t = TPC * c + j
                    if j == 0:
                        pe.wait_ge(keys_copied, c + 1)
                        pe.wait_ge(hidden_lo_ready, GS * (c + 1) - 1)
                    need(pe, y_added, t - 1)
                    tok = slice(j * P, (j + 1) * P)
                    terms = [(hidden_hi[0:r, g, tok], hidden_lo[0:r, g, tok], down_hi[0:r, g, :], down_lo[0:r, g, :])
                             for g, r in enumerate(rows)]
                    product3(pe, m.bank[DOWNB[t % 2]][:, :], terms[:-1], stop=False)
                    if j == 0:
                        pe.wait_ge(hidden_lo_ready, GS * (c + 1))
                    product3(pe, m.bank[DOWNB[t % 2]][:, :], terms[-1:], start=False).then_inc(y_done, 1)
            pe.wait_ge(rank_step, 2 * ROUNDS * NCH)
            pe.wait_ge(y_added, NT - 1)
            pe.transpose(m.bank[EB][:, 0:E], kept[:, :], m.ident[0:E, 0:E]).then_inc(kept_turned, 1)

        @block.scalar
        def _(act):
            def split(name, cols=slice(0, E)):
                act.wait_ge(w_loaded[name], 16)
                act.activation(parts[name][0][:, :, cols], raws[name][:, :, cols], ACT.Copy).then_inc(w_hi_ready[name], 1)

            split("gate_w")
            for cols in halves:
                split("sh_gate", cols)
                split("sh_up", cols)

            def hidden_to_hi(c, g):
                n, r = GS * c + g, rows[g]
                act.wait_ge(hidden_ready, n + 1)
                if g == 0:
                    need(act, y_done, TPC * c)
                act.activation(hidden_hi[0:r, g, :], hidden[n % 2][0:r, :], ACT.Copy).then_inc(hidden_hi_ready, 1)

            for c in range(NCH):
                act.wait_ge(logits_done, c + 1)
                need(act, logits_turned, c)
                act.activation(logits_e[:, :], m.bank[EB][0:E, :], ACT.Copy).then_inc(logits_copied, 1)
                for g in range(GS):
                    n, r = GS * c + g, rows[g]
                    if g == 1:
                        act.wait_ge(shifted, c + 1)
                        act.activation(logits[:, :, :], logits[:, :, :], ACT.Exp).then_inc(exp_ready, 1)
                    if g == 4:
                        act.wait_ge(keys_turned, c + 1)
                        need(act, rank_step, 2 * ROUNDS * (c - 1))
                        act.activation(ranks[c % 2][:, CAP:], m.bank[EB][0:E, :], ACT.Copy).then_inc(keys_copied, 1)
                    act.wait_ge(gate_done, n + 1)
                    need(act, hidden_ready, n - 1)
                    act.activation(silu[n % 2][0:r, :], m.bank[GATEB[n % 2]][0:r, :], ACT.Silu).then_inc(silu_ready, 1)
                    if g >= 1:
                        hidden_to_hi(c, g - 1)
                    if c == 0 and g == 1:
                        act.wait_ge(w_loaded["sh_down"], 32)
                        for p, k in TILES:
                            act.activation(down_hi[p, k, :], stage[p, k, :], ACT.Copy).then_inc(down_hi_ready, 1)
                hidden_to_hi(c, GS - 1)
                act.wait_ge(up_done, GS * (c + 1))
                if c + 1 < NCH:
                    for j in range(TPC):
                        ln.scalar_hi(act, c + 1, j)

        @block.vector
        def _(dve):
            def split(name, cols=slice(0, E)):
                hi, lo = parts[name]
                dve.wait_ge(w_hi_ready[name], 1)
                dve.tensor_tensor(lo[:, :, cols], raws[name][:, :, cols], hi[:, :, cols].bitcast(F32),
                                  ALU.subtract).then_inc(w_ready[name], 1)

            def softmax_shift(c):
                src = m.bank[TB][:, 0:TPC * E].rearrange("p (j e) -> p j e", j=TPC)
                dve.wait_ge(logits_turned, c + 1)
                dve.tensor_reduce(top[:, :], src, AX.X, ALU.max).then_inc(max_ready, 1)
                dve.wait_ge(max_ready, c + 1)
                dve.tensor_tensor(logits[:, :, :], src, top[:, :].unsqueeze(2).to_broadcast([P, TPC, E]),
                                  ALU.subtract).then_inc(shifted, 1)

            def choose(c):
                dve.wait_ge(exp_ready, c + 1)
                dve.tensor_reduce(total[:, :], logits[:, :, :], AX.X, ALU.add).then_inc(sum_ready, 1)
                dve.wait_ge(sum_ready, c + 1)
                dve.reciprocal(total[:, :], total[:, :]).then_inc(inverse_ready, 1)
                dve.wait_ge(inverse_ready, c + 1)
                need(dve, scores_stored, 16 * c)
                dve.tensor_tensor(scores[:, :, 0:E], logits[:, :, :], total[:, :].unsqueeze(2).to_broadcast([P, TPC, E]),
                                  ALU.mult).then_inc(scores_ready, 1)
                dve.wait_ge(scores_ready, c + 1)
                for j in range(TPC):
                    dve.max(best[:, j, :], scores[:, j, 0:E]).then_inc(best_ready, 1)
                dve.wait_ge(best_ready, TPC * (c + 1))
                dve.memset(best[:, :, TOPK:8], SENTINEL).then_inc(best_set, 1)
                dve.wait_ge(best_set, c + 1)
                for j in range(TPC):
                    dve.match_replace(marked[:, j, :], best[:, j, :], scores[:, j, :], -1.0).then_inc(marks_ready, 1)
                need(dve, keys_turned, c)
                for j in range(TPC):
                    t = TPC * c + j
                    dve.wait_ge(marks_ready, t + 1)
                    dve.tensor_scalar(keys[:, j, :], marked[:, j, 0:E], 0.0, key_of[:, t:t + 1],
                                      ALU.is_lt, ALU.mult).then_inc(keys_ready, 1)

            def rank(c, first, last):
                buf = ranks[c % 2]
                for i in range(first, last):
                    n = 2 * (ROUNDS * c + i)
                    if i == 0:
                        dve.wait_ge(keys_copied, c + 1)
                        need(dve, kept_moved, c)
                    need(dve, rank_step, n)
                    dve.max(kept[:, 8 * i:8 * (i + 1)], buf[:, :]).then_inc(rank_step, 1)
                    dve.wait_ge(rank_step, n + 1)
                    dve.match_replace(buf[:, :], kept[:, 8 * i:8 * (i + 1)], buf[:, :], 0.0).then_inc(rank_step, 1)
                if last == ROUNDS and c + 1 < NCH:
                    dve.wait_ge(rank_step, 2 * ROUNDS * (c + 1))
                    dve.tensor_copy(ranks[(c + 1) % 2][:, 0:CAP], kept[:, :]).then_inc(kept_moved, 1)

            def add_y(t):
                dve.wait_ge(y_done, t + 1)
                dve.tensor_tensor(m.x[:, t, :], m.bank[DOWNB[t % 2]][:, :], m.x[:, t, :], ALU.add).then_inc(y_added, 1)

            dve.memset(scores[:, :, E:], SENTINEL).then_inc(consts, 1)
            dve.memset(ranks[0][:, 0:CAP], 0.0).then_inc(consts, 1)
            dve.wait_ge(iota_set, 2)
            dve.tensor_copy(key_of[:, :], iota_i[:, :]).then_inc(consts, 1)
            dve.tensor_copy(slot_f[:, :], slot_i[:, :]).then_inc(consts, 1)
            split("gate_w")
            split("sh_gate", halves[0])
            split("sh_up", halves[0])
            dve.wait_ge(consts, 4)
            for c in range(NCH):
                softmax_shift(c)
                for g in range(GS):
                    n, r = GS * c + g, rows[g]
                    if g == 2:
                        choose(c)
                    if g == 3 and c + 1 < NCH:
                        ln.vector_stats(dve, c + 1)
                    if g == 4 and c + 1 < NCH:
                        dve.wait_ge(xn_stored, 16 * (c + 2))
                        ln.vector_normalize(dve, c + 1)
                    dve.wait_ge(silu_ready, n + 1)
                    dve.wait_ge(up_done, n + 1)
                    need(dve, hidden_lo_ready, n - 1)
                    dve.tensor_tensor(hidden[n % 2][0:r, :], silu[n % 2][0:r, :], m.bank[UPB[n % 2]][0:r, :],
                                      ALU.mult).then_inc(hidden_ready, 1)
                    if c >= 1 and g < 4:
                        rank(c - 1, 8 + 2 * g, 10 + 2 * g)
                    if g == 4:
                        rank(c, 0, 2 if c + 1 < NCH else 3)
                    if g == 5 and c + 1 == NCH:
                        rank(c, 3, 7)
                for j in range(TPC):
                    if c + 1 < NCH:
                        ln.vector_lo(dve, c + 1, j)
                        rank(c, 2 + (3 * j + 1) // 2, 2 + (3 * j + 4) // 2)
                    else:
                        rank(c, 7 + 9 * j // 4, 7 + 9 * (j + 1) // 4)
                    add_y(TPC * c + j)
            dve.wait_ge(kept_turned, 1)
            turned = m.bank[EB][:, 0:E]
            dve.tensor_scalar(empty[:, :], turned, 0.0, slot_f[:, 0:1], ALU.is_equal, ALU.mult).then_inc(empty_ready, 1)
            dve.tensor_scalar(rows_f[:, :], turned, -1.0, float(T), ALU.mult, ALU.add).then_inc(rows_ready, 1)
            dve.wait_ge(empty_ready, 1)
            dve.wait_ge(rows_ready, 1)
            dve.tensor_tensor(m.slot_rows[:, :], rows_f[:, :], empty[:, :], ALU.add).then_inc(slots_ready, 1)
            dve.wait_ge(slots_ready, 1)


def experts_phase(nc, m, a):
    arena = Arena(nc, m.after_slots + PREFETCHED * 4 * (2 * KT * F + (DOWN_FULL + 1) * D))
    R = 4
    GROUPS = E // R
    GF = (F + P - 1) // P
    rows = [min(P, F - g * P) for g in range(GF)]
    weights = m.experts + experts_weights(arena, range(PREFETCHED, R))
    w_gate, w_up, w_down = zip(*weights)
    row_in = [arena.put(f"row_in{i}", [P, 1], U32) for i in range(R)]
    row_out = [arena.put(f"row_out{i}", [P, 1], U32) for i in range(R)]
    AHEAD = R
    xg = [arena.put(f"xg{i}", [P, XS], F32) for i in range(R)]
    xt = [arena.put(f"xgt{i}", [P, KT, P], F32) for i in range(2)]
    silu = [arena.put(f"e_silu{i}", [P, F], F32) for i in range(2)]
    hidden = [arena.put(f"e_hidden{i}", [P, F], F32) for i in range(2)]
    ht_hi = [arena.put(f"e_ht_hi{i}", [P, GF, P], F32R) for i in range(2)]
    ht_lo = [arena.put(f"e_ht_lo{i}", [P, GF, P], F32R) for i in range(2)]
    down_hi = [arena.put(f"e_down_hi{i}", [P, GF, D], F32R) for i in range(2)]
    down_lo = [arena.put(f"e_down_lo{i}", [P, GF, D], F32R) for i in range(2)]
    TILES = ((slice(0, P), slice(0, GF - 1)), (slice(0, rows[GF - 1]), slice(GF - 1, GF)))
    y = [arena.put(f"e_y{i}", [P, D], F32) for i in range(2)]
    XB, GATEB, UPB, HB, YB = 0, (1, 2), (3, 4), 5, (6, 7)
    turned_hidden = m.bank[HB][:, 0:GF * P].rearrange("p (k n) -> p k n", k=GF)

    s = nc.alloc_semaphore
    gu_loaded = [s(f"gu_loaded{i}") for i in range(R)]
    down_loaded = [s(f"e_down_loaded{i}") for i in range(R)]
    gathered = [s(f"gathered{i}") for i in range(R)]
    row_in_ready, row_out_ready, x_turned, xt_ready = s("row_in_ready"), s("row_out_ready"), s("e_x_turned"), s("e_xt_ready")
    gate_done, up_done, silu_ready, hidden_ready = s("e_gate_done"), s("e_up_done"), s("e_silu_ready"), s("e_hidden_ready")
    down_hi_ready, down_ready, ht_hi_ready = s("e_down_hi_ready"), s("e_down_ready"), s("e_ht_hi_ready")
    h_turned, ht_ready, down_done, y_ready = s("e_h_turned"), s("e_ht_ready"), s("e_down_done"), s("e_y_ready")
    added, add_begun = s("expert_added"), s("expert_add_begun")

    def exists(e):
        return not isinstance(e, int) or 0 <= e < E

    def over_experts(engine, step):
        for e in range(R):
            step(e, e, 0)
        with engine.Fori(1, GROUPS - 1) as g:
            for u in range(R):
                step(g * R + u, u, g)
        for e in range(E - R, E):
            step(e, e % R, GROUPS - 1)

    with nc.Block() as block:

        @block.sync
        def _(sp):
            def step(e, u, g):
                if isinstance(e, int) and e < PREFETCHED:
                    return
                if isinstance(e, int) and e == PREFETCHED:
                    for i in range(R - 1):
                        sp.wait_ge(gathered[i], 16)
                need(sp, up_done, e - R + 1)
                need(sp, down_ready, e - R + 1)
                need(sp, add_begun, e - R + 1)
                load_gate_up(sp, a, weights[u], e, gu_loaded[u])
                load_down(sp, a, weights[u], e, down_loaded[u])
            over_experts(sp, step)

        @block.gpsimd
        def _(pool):
            def gather(e, u):
                need(pool, y_ready, e - R + 1)
                wait_apart(pool, row_in_ready, e + 1, row_in_ready)
                pool.indirect_dma_start(out=xg[u][:, :], out_offset=None, in_=a["xs"][:, :],
                                        in_offset=bass.IndirectOffsetOnAxis(ap=row_in[u][:, :], axis=0)).then_inc(gathered[u], 16)

            def step(e, u, g):
                pool.wait_ge(row_out_ready, e + 1)
                pool.wait_ge(y_ready, e + 1)
                wait_apart(pool, added, 16 * e, row_out_ready)
                pool.indirect_dma_start(out=a["out"][:, :], out_offset=bass.IndirectOffsetOnAxis(ap=row_out[u][:, :], axis=0),
                                        in_=y[u % 2][:, :], in_offset=None, compute_op=ALU.add,
                                        engine_sem=add_begun).then_inc(added, 16)
                if exists(e + AHEAD):
                    gather(e + AHEAD, (u + AHEAD) % R)
            for e in range(AHEAD):
                gather(e, e)
            over_experts(pool, step)
            pool.wait_ge(added, 16 * E)

        @block.tensor
        def _(pe):
            def turn_x(e, u, g):
                pe.wait_ge(gathered[u], 16 * (g + 1))
                need(pe, xt_ready, e)
                for k in range(KT):
                    last = pe.transpose(m.bank[XB][:, k * P:(k + 1) * P], xg[u][:, k:D:KT], m.ident[:, :])
                last.then_inc(x_turned, 1)

            def down(e, u, g):
                pe.wait_ge(ht_ready, e + 1)
                pe.wait_ge(down_ready, e + 1)
                need(pe, y_ready, e - 1)
                b = u % 2
                product3(pe, m.bank[YB[b]][:, :],
                         [(ht_hi[b][0:r, k, :], ht_lo[b][0:r, k, :], down_hi[b][0:r, k, :], down_lo[b][0:r, k, :])
                          for k, r in enumerate(rows)]).then_inc(down_done, 1)

            def step(e, u, g):
                if exists(e + 1):
                    turn_x(e + 1, (u + 1) % R, g if u < R - 1 else g + 1)
                pe.wait_ge(xt_ready, e + 1)
                need(pe, gu_loaded[u], 32 * (g if u < PREFETCHED else g + 1))
                need(pe, hidden_ready, e - 1)
                for w, bank, done in ((w_gate, GATEB, gate_done), (w_up, UPB, up_done)):
                    for k in range(KT):
                        last = pe.matmul(m.bank[bank[u % 2]][:, 0:F], xt[u % 2][:, k, :], w[u][:, k, :],
                                         start=(k == 0), stop=(k == KT - 1))
                    last.then_inc(done, 1)
                if exists(e - 1):
                    down(e - 1, (u - 1) % R, g if u else g - 1)
                pe.wait_ge(hidden_ready, e + 1)
                need(pe, ht_ready, e)
                for k in range(GF):
                    r = rows[k]
                    last = pe.transpose(m.bank[HB][0:r, k * P:(k + 1) * P], hidden[u % 2][:, k * P:k * P + r], m.ident[:, :])
                last.then_inc(h_turned, 1)

            turn_x(0, 0, 0)
            over_experts(pe, step)
            down(E - 1, R - 1, GROUPS - 1)

        @block.scalar
        def _(act):
            def weigh(e, u):
                act.wait_ge(down_done, e + 1)
                need(act, added, 16 * (e - 1))
                act.activation(y[u % 2][:, :], m.bank[YB[u % 2]][:, :], ACT.Copy,
                               scale=xg[u][:, bass.ds(D + e, 1)]).then_inc(y_ready, 1)

            def step(e, u, g):
                act.wait_ge(gate_done, e + 1)
                need(act, hidden_ready, e - 1)
                act.activation(silu[u % 2][:, :], m.bank[GATEB[u % 2]][:, 0:F], ACT.Silu).then_inc(silu_ready, 1)
                need(act, down_loaded[u], 32 * (g if u < PREFETCHED else g + 1))
                need(act, down_done, e - 1)
                for p, k in TILES:
                    last = act.activation(down_hi[u % 2][p, k, :], w_down[u][p, k, :], ACT.Copy)
                last.then_inc(down_hi_ready, 1)
                if exists(e - 1):
                    weigh(e - 1, (u - 1) % R)
                act.wait_ge(h_turned, e + 1)
                for p, k in TILES:
                    last = act.activation(ht_hi[u % 2][p, k, :], turned_hidden[p, k, :], ACT.Copy)
                last.then_inc(ht_hi_ready, 1)
            over_experts(act, step)
            weigh(E - 1, R - 1)

        @block.vector
        def _(dve):
            def copy_row_in(e, u, g):
                if not isinstance(e, int) or e >= R:
                    wait_apart(dve, gathered[u], 16 * g, row_in_ready)
                dve.tensor_copy(row_in[u][:, :], m.slot_rows[:, bass.ds(e, 1)]).then_inc(row_in_ready, 1)

            def copy_row_out(e, u):
                wait_apart(dve, added, 16 * (e - R + 1), row_in_ready)
                dve.tensor_copy(row_out[u][:, :], m.slot_rows[:, bass.ds(e, 1)]).then_inc(row_out_ready, 1)

            def copy_x(e, u):
                dve.wait_ge(x_turned, e + 1)
                need(dve, up_done, e - 1)
                dve.tensor_copy(xt[u % 2][:, :, :], m.bank[XB][:, :].rearrange("p (k n) -> p k n", k=KT)).then_inc(xt_ready, 1)

            def step(e, u, g):
                if exists(e + 1):
                    copy_x(e + 1, (u + 1) % R)
                if exists(e + AHEAD):
                    copy_row_in(e + AHEAD, (u + AHEAD) % R, g + (u + AHEAD) // R)
                copy_row_out(e, u)
                dve.wait_ge(silu_ready, e + 1)
                dve.wait_ge(up_done, e + 1)
                need(dve, h_turned, e - 1)
                dve.tensor_tensor(hidden[u % 2][:, :], silu[u % 2][:, :], m.bank[UPB[u % 2]][:, 0:F],
                                  ALU.mult).then_inc(hidden_ready, 1)
                dve.wait_ge(down_hi_ready, e + 1)
                for p, k in TILES:
                    last = dve.tensor_tensor(down_lo[u % 2][p, k, :], w_down[u][p, k, :],
                                             down_hi[u % 2][p, k, :].bitcast(F32), ALU.subtract)
                last.then_inc(down_ready, 1)
                dve.wait_ge(ht_hi_ready, e + 1)
                for p, k in TILES:
                    last = dve.tensor_tensor(ht_lo[u % 2][p, k, :], turned_hidden[p, k, :],
                                             ht_hi[u % 2][p, k, :].bitcast(F32), ALU.subtract)
                last.then_inc(ht_ready, 1)

            for e in range(AHEAD):
                copy_row_in(e, e, 0)
            copy_x(0, 0)
            over_experts(dve, step)


PHASES = [qkv_phase, attention_phase, ffn_phase, recurrence_phase, router_phase, experts_phase]


def build(nc, a):
    m = setup_memory(nc, a)
    for phase in PHASES:
        free = list(nc.free_semaphores)
        phase(nc, m, a)
        left = set(nc.free_semaphores)
        nc.clear_and_free_semaphores([i for i in free if i not in left])
        nc.all_engine_barrier()


def kernel(**inputs):
    import numpy as np
    import concourse.bacc as bacc
    from concourse.bass_utils import run_bass_kernel_spmd

    def np_of(name):
        return np.asarray(inputs[name])

    def nibble_order(w, axis):
        w = np.moveaxis(w, axis, 0)
        w = w.reshape(w.shape[0] // P, 16, 8, *w.shape[1:]).swapaxes(1, 2).reshape(w.shape)
        return np.moveaxis(w, 0, axis)

    def columns(words):
        return words.reshape(-1, 16, words.shape[1]).swapaxes(0, 1).reshape(16, -1)

    gu, gus = np_of("L0_ffn_gate_up_packed"), np_of("L0_ffn_gate_up_scales")
    arrays = {
        "x": np_of("L0_attn_x").reshape(T, D),
        "wqkv": np_of("L0_attn_Wqkv"),
        "bqkv": np_of("L0_attn_bqkv"),
        "wo": np_of("L0_attn_Wo"),
        "bo": np_of("L0_attn_bo"),
        "fp4_words": np.tile(np.concatenate([columns(nibble_order(gu, 0).T),
                                             columns(np_of("L0_ffn_down_packed").T)], 1), (8, 1)),
        "fp4_scales": np.concatenate([nibble_order(gus, 1).ravel(), np_of("L0_ffn_down_scales").ravel()]),
        "w_in": np_of("L1_attn_W_in").T,
        "w_out": np_of("L1_attn_W_out").T,
        "decay": np_of("L1_attn_decay"),
        "b1": np_of("L1_attn_bias"),
        "gate_w": np_of("L1_ffn_gate_w").T,
        "w_gate": np_of("L1_ffn_w_gate"),
        "w_up": np_of("L1_ffn_w_up"),
        "w_down": np_of("L1_ffn_w_down"),
        "sh_gate": np_of("L1_ffn_sh_gate").T,
        "sh_up": np_of("L1_ffn_sh_up").T,
        "sh_down": np_of("L1_ffn_sh_down").T,
    }
    nc = bacc.Bacc("TRN2", target_bir_lowering=False, num_devices=1)
    a, maps = {}, {}
    for name, v in arrays.items():
        v = np.ascontiguousarray(v)
        maps[f"in_{name}"] = v
        a[name] = nc.dram_tensor(f"in_{name}", v.shape, mybir.dt.from_np(v.dtype), kind="ExternalInput").ap()
    a["out"] = nc.dram_tensor("out_x", (T + P, D), F32, kind="ExternalOutput").ap()
    a["qk"] = nc.dram_tensor("qk_parts", (2, B, 2, D, S), F32).ap()
    a["fp4_out"] = nc.dram_tensor("fp4_out", (3, P, GU_COLS + DOWN_COLS), F32).ap()
    a["xs"] = nc.dram_tensor("expert_rows", (T + P, XS), F32).ap()
    build(nc, a)
    r = run_bass_kernel_spmd(nc, [maps], core_ids=[0])
    return r.results[0]["out_x"][:T].reshape(B, S, D)
```
